# Optimizing a Trainium2 kernel written in Bass

```python
import numpy as np
import jax
import jax.numpy as jnp

def _softmax(x, axis=-1):
    return jax.nn.softmax(x, axis=axis)

def _gelu(x):
    return jax.nn.gelu(x, approximate=True)

def _silu(x):
    return jax.nn.silu(x)

def _sigmoid(x):
    return jax.nn.sigmoid(x)

def _layernorm(x, axis=-1, eps=1e-05):
    m = jnp.mean(x, axis=axis, keepdims=True)
    v = jnp.var(x, axis=axis, keepdims=True)
    return (x - m) / jnp.sqrt(v + eps)

def _scatter_add(tgt, idx, src, axis=0):
    return tgt.at[idx].add(src)

def _segment_sum(src, seg, n):
    return jax.ops.segment_sum(src, seg, n)
kernel_name = 'mk_macaron_d2_jaxref_r8_f82ae6'

def setup_inputs(seed: int=0):
    np.random.seed(seed)
    _w = jnp.asarray

    def _L0_attn_setup():
        import jax, jax.numpy as jnp
        import numpy as np
        B, N, DIM, H = (4, 512, 128, 16)
        HD = DIM // H
        SCALE = HD ** (-0.5)

        def _heads(t, bsz, ntok):
            return t.reshape(bsz, ntok, H, HD).transpose(0, 2, 1, 3)

        def _fwd(x, q_w1, q_b1, q_w2, q_b2, k_w1, k_b1, k_w2, k_b2, v_w, v_b, g_w, g_b, p_w, p_b):
            bsz, ntok, dim = x.shape
            gelu = lambda t: jax.nn.gelu(t, approximate=False)
            q = _heads(jax.nn.softplus(gelu(x @ q_w1.T + q_b1) @ q_w2.T + q_b2), bsz, ntok)
            k = _heads(jax.nn.softplus(gelu(x @ k_w1.T + k_b1) @ k_w2.T + k_b2), bsz, ntok)
            v = _heads(gelu(x @ v_w.T + v_b), bsz, ntok)
            g = _heads(gelu(x @ g_w.T + g_b), bsz, ntok)
            z = jnp.einsum('bhcn,bhc->bhn', q, k.sum(axis=-1)) * SCALE
            z = 1.0 / (z + dim)
            A = jnp.einsum('bhcn,bhcm->bhnm', q, k)
            out = jnp.einsum('bhnm,bhdm->bhdn', A, v) * SCALE
            out = (out + v) * z[:, :, None, :]
            out = out.reshape(bsz, ntok, dim)
            out = out * g.reshape(bsz, ntok, dim)
            return out @ p_w.T + p_b
        key = jax.random.key(seed)
        ks = jax.random.split(key, 16)
        w = lambda k: jax.random.normal(k, (DIM, DIM), jnp.float32) * 0.02
        b = lambda k: jax.random.normal(k, (DIM,), jnp.float32) * 0.02
        return {'x': jax.random.normal(ks[0], (B, N, DIM), jnp.float32), 'q_w1': w(ks[1]), 'q_b1': b(ks[2]), 'q_w2': w(ks[3]), 'q_b2': b(ks[4]), 'k_w1': w(ks[5]), 'k_b1': b(ks[6]), 'k_w2': w(ks[7]), 'k_b2': b(ks[8]), 'v_w': w(ks[9]), 'v_b': b(ks[10]), 'g_w': w(ks[11]), 'g_b': b(ks[12]), 'p_w': w(ks[13]), 'p_b': b(ks[14])}
    _L0_attn_in = _L0_attn_setup()

    def _L0_ffn_setup():
        import jax, jax.numpy as jnp
        import numpy as np
        from jax import lax
        D_MODEL = 128
        D_FF = 512
        NUM_EXPERTS = 24
        TOP_K = 2
        B, S = (2, 256)
        key = jax.random.key(seed)
        ks = jax.random.split(key, 5)
        x = jax.random.normal(ks[0], (B, S, D_MODEL), dtype=jnp.float32)
        gate_w = jax.random.normal(ks[1], (D_MODEL, NUM_EXPERTS), dtype=jnp.float32) * 0.02
        gate_b = jnp.zeros((NUM_EXPERTS,), dtype=jnp.float32)
        w1 = jax.random.normal(ks[2], (NUM_EXPERTS, D_MODEL, D_FF), dtype=jnp.float32) * 0.02
        b1 = jnp.zeros((NUM_EXPERTS, D_FF), dtype=jnp.float32)
        w2 = jax.random.normal(ks[3], (NUM_EXPERTS, D_FF, D_MODEL), dtype=jnp.float32) * 0.02
        b2 = jnp.zeros((NUM_EXPERTS, D_MODEL), dtype=jnp.float32)
        return {'x': x, 'gate_w': gate_w, 'gate_b': gate_b, 'w1': w1, 'b1': b1, 'w2': w2, 'b2': b2}
    _L0_ffn_in = _L0_ffn_setup()

    def _L1_attn_setup():
        import jax, jax.numpy as jnp
        import numpy as np
        DIM = 128
        SEQ = 512
        BATCH = 4
        ROPE_BASE = 10000.0

        def rotate_half(x):
            x_even = x[..., 0::2]
            x_odd = x[..., 1::2]
            return jnp.stack((-x_odd, x_even), axis=-1).reshape(x.shape)

        def rope_tables(seq_len, dim, base=ROPE_BASE, dtype=jnp.float32):
            pos = jnp.arange(seq_len, dtype=jnp.float32)[:, None]
            inv_freq = 1.0 / base ** (jnp.arange(0, dim, 2, dtype=jnp.float32) / dim)
            freqs = pos * inv_freq
            cos = jnp.repeat(jnp.cos(freqs), 2, axis=-1).astype(dtype)
            sin = jnp.repeat(jnp.sin(freqs), 2, axis=-1).astype(dtype)
            return (cos, sin)
        key = jax.random.key(seed)
        kx, kq, kk, kv = jax.random.split(key, 4)
        s = 1.0 / np.sqrt(DIM)
        return {'x': jax.random.normal(kx, (BATCH, SEQ, DIM), dtype=jnp.float32), 'wq': jax.random.normal(kq, (DIM, DIM), dtype=jnp.float32) * s, 'wk': jax.random.normal(kk, (DIM, DIM), dtype=jnp.float32) * s, 'wv': jax.random.normal(kv, (DIM, DIM), dtype=jnp.float32) * s}
    _L1_attn_in = _L1_attn_setup()

    def _L1_ffn_setup():
        import jax, jax.numpy as jnp
        import numpy as np
        D = 128
        H = 256
        E = 8
        TOP_K = 2
        N_SHARED = 1
        B, S = (2, 128)
        key = jax.random.key(seed)
        ks = jax.random.split(key, 12)
        sc = 0.02
        return {'hidden': jax.random.normal(ks[0], (B, S, D), jnp.float32), 'router_w': jax.random.normal(ks[1], (D, E), jnp.float32) * sc, 'router_b': jnp.zeros((E,), jnp.float32), 'sw1': jax.random.normal(ks[2], (D, H), jnp.float32) * sc, 'sb1': jnp.zeros((H,), jnp.float32), 'sw2': jax.random.normal(ks[3], (H, D), jnp.float32) * sc, 'sb2': jnp.zeros((D,), jnp.float32), 'rw1': jax.random.normal(ks[4], (E, D, H), jnp.float32) * sc, 'rb1': jnp.zeros((E, H), jnp.float32), 'rw2': jax.random.normal(ks[5], (E, H, D), jnp.float32) * sc, 'rb2': jnp.zeros((E, D), jnp.float32)}
    _L1_ffn_in = _L1_ffn_setup()
    _d = {'L0_attn_x': _L0_attn_in['x'], 'L0_attn_q_w1': _L0_attn_in['q_w1'], 'L0_attn_q_b1': _L0_attn_in['q_b1'], 'L0_attn_q_w2': _L0_attn_in['q_w2'], 'L0_attn_q_b2': _L0_attn_in['q_b2'], 'L0_attn_k_w1': _L0_attn_in['k_w1'], 'L0_attn_k_b1': _L0_attn_in['k_b1'], 'L0_attn_k_w2': _L0_attn_in['k_w2'], 'L0_attn_k_b2': _L0_attn_in['k_b2'], 'L0_attn_v_w': _L0_attn_in['v_w'], 'L0_attn_v_b': _L0_attn_in['v_b'], 'L0_attn_g_w': _L0_attn_in['g_w'], 'L0_attn_g_b': _L0_attn_in['g_b'], 'L0_attn_p_w': _L0_attn_in['p_w'], 'L0_attn_p_b': _L0_attn_in['p_b'], 'L0_ffn_gate_w': _L0_ffn_in['gate_w'], 'L0_ffn_gate_b': _L0_ffn_in['gate_b'], 'L0_ffn_w1': _L0_ffn_in['w1'], 'L0_ffn_b1': _L0_ffn_in['b1'], 'L0_ffn_w2': _L0_ffn_in['w2'], 'L0_ffn_b2': _L0_ffn_in['b2'], 'L1_attn_wq': _L1_attn_in['wq'], 'L1_attn_wk': _L1_attn_in['wk'], 'L1_attn_wv': _L1_attn_in['wv'], 'L1_ffn_router_w': _L1_ffn_in['router_w'], 'L1_ffn_router_b': _L1_ffn_in['router_b'], 'L1_ffn_sw1': _L1_ffn_in['sw1'], 'L1_ffn_sb1': _L1_ffn_in['sb1'], 'L1_ffn_sw2': _L1_ffn_in['sw2'], 'L1_ffn_sb2': _L1_ffn_in['sb2'], 'L1_ffn_rw1': _L1_ffn_in['rw1'], 'L1_ffn_rb1': _L1_ffn_in['rb1'], 'L1_ffn_rw2': _L1_ffn_in['rw2'], 'L1_ffn_rb2': _L1_ffn_in['rb2']}
    _x0 = _d['L0_attn_x']
    _d['L0_attn_x'] = jax.random.normal(jax.random.fold_in(jax.random.key(seed), 1), (8, 512, 128), dtype=_x0.dtype)
    del _x0
    return _d

def reference(L0_attn_x, L0_attn_q_w1, L0_attn_q_b1, L0_attn_q_w2, L0_attn_q_b2, L0_attn_k_w1, L0_attn_k_b1, L0_attn_k_w2, L0_attn_k_b2, L0_attn_v_w, L0_attn_v_b, L0_attn_g_w, L0_attn_g_b, L0_attn_p_w, L0_attn_p_b, L0_ffn_gate_w, L0_ffn_gate_b, L0_ffn_w1, L0_ffn_b1, L0_ffn_w2, L0_ffn_b2, L1_attn_wq, L1_attn_wk, L1_attn_wv, L1_ffn_router_w, L1_ffn_router_b, L1_ffn_sw1, L1_ffn_sb1, L1_ffn_sw2, L1_ffn_sb2, L1_ffn_rw1, L1_ffn_rb1, L1_ffn_rw2, L1_ffn_rb2):

    def _L0_attn_ref(x, q_w1, q_b1, q_w2, q_b2, k_w1, k_b1, k_w2, k_b2, v_w, v_b, g_w, g_b, p_w, p_b):
        import jax, jax.numpy as jnp
        import numpy as np
        B, N, DIM, H = (4, 512, 128, 16)
        HD = DIM // H
        SCALE = HD ** (-0.5)

        def _heads(t, bsz, ntok):
            return t.reshape(bsz, ntok, H, HD).transpose(0, 2, 1, 3)

        def _fwd(x, q_w1, q_b1, q_w2, q_b2, k_w1, k_b1, k_w2, k_b2, v_w, v_b, g_w, g_b, p_w, p_b):
            bsz, ntok, dim = x.shape
            gelu = lambda t: jax.nn.gelu(t, approximate=False)
            q = _heads(jax.nn.softplus(gelu(x @ q_w1.T + q_b1) @ q_w2.T + q_b2), bsz, ntok)
            k = _heads(jax.nn.softplus(gelu(x @ k_w1.T + k_b1) @ k_w2.T + k_b2), bsz, ntok)
            v = _heads(gelu(x @ v_w.T + v_b), bsz, ntok)
            g = _heads(gelu(x @ g_w.T + g_b), bsz, ntok)
            z = jnp.einsum('bhcn,bhc->bhn', q, k.sum(axis=-1)) * SCALE
            z = 1.0 / (z + dim)
            A = jnp.einsum('bhcn,bhcm->bhnm', q, k)
            out = jnp.einsum('bhnm,bhdm->bhdn', A, v) * SCALE
            out = (out + v) * z[:, :, None, :]
            out = out.reshape(bsz, ntok, dim)
            out = out * g.reshape(bsz, ntok, dim)
            return out @ p_w.T + p_b
        return _fwd(x, q_w1, q_b1, q_w2, q_b2, k_w1, k_b1, k_w2, k_b2, v_w, v_b, g_w, g_b, p_w, p_b)

    def _L0_ffn_ref(x, gate_w, gate_b, w1, b1, w2, b2):
        import jax, jax.numpy as jnp
        import numpy as np
        from jax import lax
        D_MODEL = 128
        D_FF = 512
        NUM_EXPERTS = 24
        TOP_K = 2
        B, S = (2, 256)
        b, s, d = x.shape
        t = b * s
        xf = x.reshape(t, d)
        scores = xf @ gate_w + gate_b
        top_val, top_idx = lax.top_k(scores, TOP_K)
        prob = jax.nn.softmax(top_val, axis=-1)
        combine = jnp.zeros((t, NUM_EXPERTS), dtype=x.dtype)
        combine = combine.at[jnp.arange(t)[:, None], top_idx].add(prob)

        def body(acc, expert):
            w1e, b1e, w2e, b2e, ce = expert
            h = jax.nn.gelu(xf @ w1e + b1e, approximate=False)
            y = h @ w2e + b2e
            return (acc + ce[:, None] * y, None)
        out, _ = lax.scan(body, jnp.zeros_like(xf), (w1, b1, w2, b2, combine.T))
        return out.reshape(b, s, d)

    def _L1_attn_ref(x, wq, wk, wv):
        import jax, jax.numpy as jnp
        import numpy as np
        DIM = 128
        SEQ = 512
        BATCH = 4
        ROPE_BASE = 10000.0

        def rotate_half(x):
            x_even = x[..., 0::2]
            x_odd = x[..., 1::2]
            return jnp.stack((-x_odd, x_even), axis=-1).reshape(x.shape)

        def rope_tables(seq_len, dim, base=ROPE_BASE, dtype=jnp.float32):
            pos = jnp.arange(seq_len, dtype=jnp.float32)[:, None]
            inv_freq = 1.0 / base ** (jnp.arange(0, dim, 2, dtype=jnp.float32) / dim)
            freqs = pos * inv_freq
            cos = jnp.repeat(jnp.cos(freqs), 2, axis=-1).astype(dtype)
            sin = jnp.repeat(jnp.sin(freqs), 2, axis=-1).astype(dtype)
            return (cos, sin)
        q = jnp.einsum('bsd,ed->bse', x, wq)
        k = jnp.einsum('bsd,ed->bse', x, wk)
        v = jnp.einsum('bsd,ed->bse', x, wv)
        seq_len, dim = (q.shape[-2], q.shape[-1])
        cos, sin = rope_tables(seq_len, dim, dtype=q.dtype)
        q = q * cos + rotate_half(q) * sin
        k = k * cos + rotate_half(k) * sin
        scale = 1.0 / jnp.sqrt(jnp.asarray(dim, dtype=q.dtype))
        scores = jnp.einsum('bqd,bkd->bqk', q, k) * scale
        mask = jnp.triu(jnp.ones((seq_len, seq_len), dtype=bool), k=1)
        scores = jnp.where(mask, jnp.asarray(-jnp.inf, dtype=scores.dtype), scores)
        weights = jax.nn.softmax(scores, axis=-1)
        return jnp.einsum('bqk,bkd->bqd', weights, v)

    def _L1_ffn_ref(hidden, router_w, router_b, sw1, sb1, sw2, sb2, rw1, rb1, rw2, rb2):
        import jax, jax.numpy as jnp
        import numpy as np
        D = 128
        H = 256
        E = 8
        TOP_K = 2
        N_SHARED = 1
        B, S = (2, 128)
        b, s, d = hidden.shape
        T = b * s
        flat = hidden.reshape(T, d)
        router_logits = flat @ router_w + router_b
        router_probs = jax.nn.softmax(router_logits, axis=-1)
        topk_probs, topk_idx = jax.lax.top_k(router_probs, TOP_K)
        weights = jnp.zeros_like(router_probs).at[jnp.arange(T)[:, None], topk_idx].add(topk_probs)
        sh = jax.nn.gelu(flat @ sw1 + sb1, approximate=False)
        shared_out = (sh @ sw2 + sb2) / N_SHARED
        h1 = jax.nn.gelu(jnp.einsum('td,edh->teh', flat, rw1) + rb1[None], approximate=False)
        expert_out = jnp.einsum('teh,ehd->ted', h1, rw2) + rb2[None]
        mixed = jnp.einsum('ted,te->td', expert_out, weights)
        return (shared_out + mixed).reshape(b, s, d)
    x = L0_attn_x
    x = x + 0.5 * _L0_ffn_ref(_layernorm(x, axis=-1), L0_ffn_gate_w, L0_ffn_gate_b, L0_ffn_w1, L0_ffn_b1, L0_ffn_w2, L0_ffn_b2)
    x = x + _L0_attn_ref(_layernorm(x, axis=-1), L0_attn_q_w1, L0_attn_q_b1, L0_attn_q_w2, L0_attn_q_b2, L0_attn_k_w1, L0_attn_k_b1, L0_attn_k_w2, L0_attn_k_b2, L0_attn_v_w, L0_attn_v_b, L0_attn_g_w, L0_attn_g_b, L0_attn_p_w, L0_attn_p_b)
    x = x + 0.5 * _L0_ffn_ref(_layernorm(x, axis=-1), L0_ffn_gate_w, L0_ffn_gate_b, L0_ffn_w1, L0_ffn_b1, L0_ffn_w2, L0_ffn_b2)
    x = x + 0.5 * _L1_ffn_ref(_layernorm(x, axis=-1), L1_ffn_router_w, L1_ffn_router_b, L1_ffn_sw1, L1_ffn_sb1, L1_ffn_sw2, L1_ffn_sb2, L1_ffn_rw1, L1_ffn_rb1, L1_ffn_rw2, L1_ffn_rb2)
    x = x + _L1_attn_ref(_layernorm(x, axis=-1), L1_attn_wq, L1_attn_wk, L1_attn_wv)
    x = x + 0.5 * _L1_ffn_ref(_layernorm(x, axis=-1), L1_ffn_router_w, L1_ffn_router_b, L1_ffn_sw1, L1_ffn_sb1, L1_ffn_sw2, L1_ffn_sb2, L1_ffn_rw1, L1_ffn_rb1, L1_ffn_rw2, L1_ffn_rb2)
    return x

_drawn_inputs = setup_inputs


def setup_inputs(seed=0):
    import zlib

    import numpy as np

    out = dict(_drawn_inputs(seed))
    spreads = {'L0_ffn_gate_b': (0.0, 0.1),
     'L0_ffn_b1': (0.0, 0.433),
     'L0_ffn_b2': (0.0, 0.1),
     'L1_ffn_router_b': (0.0, 0.559),
     'L1_ffn_sb1': (0.0, 0.432),
     'L1_ffn_sb2': (0.0, 0.1),
     'L1_ffn_rb1': (0.0, 0.8),
     'L1_ffn_rb2': (0.0, 0.348)}
    factors = {'L0_attn_q_w1': 8.0,
     'L0_attn_q_b1': 32.605,
     'L0_attn_q_w2': 8.0,
     'L0_attn_q_b2': 28.436,
     'L0_attn_k_w1': 8.0,
     'L0_attn_k_b1': 8.0,
     'L0_attn_k_w2': 8.0,
     'L0_attn_k_b2': 8.0,
     'L0_attn_v_w': 8.0,
     'L0_attn_v_b': 8.0,
     'L0_attn_g_w': 8.0,
     'L0_attn_g_b': 8.0,
     'L0_attn_p_w': 8.0,
     'L1_ffn_router_w': 2.821,
     'L1_ffn_rw1': 6.747,
     'L1_ffn_rw2': 5.897,
     'L0_attn_p_b': 2.845}
    for name, (base, spread) in spreads.items():
        noise = np.random.default_rng([zlib.crc32(name.encode()), seed]).standard_normal(out[name].shape)
        drawn = base * np.exp(spread * noise) if base else spread * noise
        out[name] = jnp.asarray(drawn.astype(out[name].dtype))
    for name, factor in factors.items():
        out[name] = (out[name] * factor).astype(out[name].dtype)
    return out
```

```python
from contextlib import ExitStack

import concourse.bass as bass
import numpy as np
from concourse import mybir

F32 = mybir.dt.float32
F16 = mybir.dt.float16
I32 = mybir.dt.int32
ALU = mybir.AluOpType
ACT = mybir.ActivationFunctionType
AX = mybir.AxisListType
VECTOR, SYNC = "vector", "sync"
ENGINE_TYPE = {VECTOR: mybir.EngineType.DVE, SYNC: mybir.EngineType.SP}

P = 128
D = 128
BATCHES, SEQ = 8, 512
STREAMS = 2
SB = BATCHES // STREAMS
BT = SEQ // P
NT = SB * BT
TOP_K = 2
EPS = 1e-5
RSQRT_GUESS = 0x5F3759DF
NEWTON_STEPS = 3

HEADS = 16
HEAD_DIM = D // HEADS
HEAD_SCALE = HEAD_DIM ** -0.5
ATTN_SCALE = D ** -0.5

X_SCALE = 32.0
W_SCALE = 32.0
SEL_VALUE = 4.0
LOW_ROW = 32


class Layer:

    def __init__(self, name, experts, hidden):
        self.name, self.E, self.H = name, experts, hidden
        self.chunks = hidden // P
        pairs = NT * P * TOP_K
        bound = (pairs - experts) // P + experts
        self.tiles = -(-bound // BT) * BT
        self.unit = SEQ // hidden
        self.block = hidden + P // 2


L0 = Layer("l0", 24, 512)
L1 = Layer("l1", 8, 256)
MAX_TILES = max(L0.tiles, L1.tiles)

MATS = ["q1", "k1", "v", "g", "q2", "k2", "p", "wq", "wq_swap", "wk", "wk_swap", "wv"]


def columns(widths):
    at, out = 0, {}
    for name, n in widths:
        out[name] = (at, at + n)
        at += n
    return out, at


WCOL, WCOLS = columns([(m, D) for m in MATS] + [
    ("gate_w0", L0.E), ("gate_w1", L1.E), ("gate_b0", L0.E), ("gate_b1", L1.E),
    ("sw1", L1.H), ("sw2", L1.chunks * D), ("q_b1", 1), ("k_b1", 1), ("v_b", 1), ("g_b", 1), ("sb1", L1.chunks)])
BCOL, BCOLS = columns([("b1_0", L0.H), ("b1_1", L1.H), ("b2_0", D), ("b2_1", D),
                       ("q_b2", D), ("k_b2", D), ("p_b", D), ("sb2", D)])
HIDDEN_BIAS_COLS = L0.H + L1.H
CCOL, CCOLS = columns([("ident", P), ("heads", D), ("causal", P), ("cos", SEQ), ("sin", SEQ),
                       ("carry", L0.E * NT), ("rev0", L0.E), ("rev1", L1.E), ("iota", 1), ("one", 1)])
HCOL, HCOLS = columns([("ident", P), ("before", P), ("ones", P), ("select", L0.E * P)])
HALF_KEPT = HCOL["select"][0]


class Token:

    def __init__(self, sem, value):
        self.sem, self.value = sem, value


class Queues:

    def __init__(self, nc, ctx):
        self.nc, self.ctx = nc, ctx
        self.sems, self.count = {}, {}
        self.engines = {"tensor": nc.tensor, "vector": nc.vector, "scalar": nc.scalar, "gpsimd": nc.gpsimd, "sync": nc.sync}
        self.waited = {e: {} for e in self.engines}

    def put(self, engine, work, after, signal=None, by=1):
        waits = []
        seen = self.waited[engine]
        best = {}
        for t in after:
            best[t.sem] = max(best.get(t.sem, 0), t.value)
        for name, value in best.items():
            if seen.get(name, 0) < value:
                seen[name] = value
                waits.append((name, value))
        if signal is not None:
            if signal not in self.sems:
                self.sems[signal] = self.ctx.enter_context(self.nc.semaphore(signal))
                self.count[signal] = 0
            self.count[signal] += by
        eng = self.engines[engine]
        for name, value in waits:
            eng.wait_ge(self.sems[name], value)
        last = work(eng)
        if signal is not None:
            last.then_inc(self.sems[signal], by)
        return Token(signal, self.count[signal]) if signal is not None else None


class Slot:
    def __init__(self, ap, name):
        self.ap, self.name, self.ready = ap, name, []


class Slots:

    def __init__(self, aps, name):
        self.free = [Slot(ap, f"{name}{i}") for i, ap in enumerate(aps)]

    def take(self):
        return self.free.pop(0)

    def release(self, slot, *tokens):
        slot.ready = list(tokens)
        self.free.append(slot)


def macaron_program(nc, x_in, w_in, bias_in, const_in, half_in, w1_0, w2_0, w1_1, w2_1, x_out):
    with ExitStack() as ctx:
        def sb(name, shape, dt):
            return ctx.enter_context(nc.sbuf_tensor(name, shape, dt))

        def bank(name, shape=(P, SEQ), dt=F32):
            return ctx.enter_context(nc.psum_tensor(name, list(shape), dt))

        q = Queues(nc, ctx)
        put = q.put

        x_res = [sb(f"x_res{s}", [P, NT, D], F32) for s in range(STREAMS)]
        weights = sb("weights", [P, WCOLS], F32)
        const = sb("const", [P, CCOLS], F32)
        half = sb("half", [P, HALF_KEPT], F16)
        bias = sb("bias", [P, BCOLS], F16)
        blocks = {layer: sb(f"blocks_{layer.name}", [P, layer.E * layer.block], F32) for layer in (L0, L1)}
        expert_block = sb("expert_block", [P, 3 * STREAMS, max(l.block * l.unit for l in (L0, L1))], F32)
        slot_index = [sb(f"slot_index{s}", [P, TOP_K, NT], I32) for s in range(STREAMS)]
        share = [sb(f"share{s}", [P, TOP_K, NT], F32) for s in range(STREAMS)]
        tile_expert = [sb(f"tile_expert{s}", [1, 2, MAX_TILES], I32) for s in range(STREAMS)]
        NWORK, NSMALL = 30, 12
        work_mem = sb("work_mem", [P, NWORK, SEQ], F32)
        small_mem = sb("small_mem", [P, NSMALL, 96], F32)

        work = Slots([work_mem[:, i, :] for i in range(NWORK)], "work")
        block_slots = [Slots([expert_block[:, 3 * s + i, :] for i in range(3)], f"expert_block{s}_") for s in range(STREAMS)]
        small = Slots([small_mem[:, i, :] for i in range(NSMALL)], "small")
        banks = Slots([bank(f"bank{i}")[:, :] for i in range(3)], "bank")
        hidden_banks = Slots([bank(f"hidden_bank{i}")[:, :] for i in range(2)], "hidden_bank")
        out_banks = Slots([bank(f"out_bank{i}")[:, :] for i in range(2)], "out_bank")
        turn_banks = Slots([bank("turn_bank", (P, 2 * SEQ), F16)[:, :]], "turn_bank")

        rows_dram = [nc.dram_tensor(f"rows{s}", [MAX_TILES * P, 2 * D], F16, kind="Internal").ap() for s in range(STREAMS)]
        y_dram = [nc.dram_tensor(f"y{s}", [MAX_TILES * P, D], F32, kind="Internal").ap() for s in range(STREAMS)]
        heads_dram = [nc.dram_tensor(f"heads{i}", [D, SEQ], F32, kind="Internal").ap() for i in range(BATCHES)]

        def wcol(name):
            return weights[:, WCOL[name][0]:WCOL[name][1]]

        def bcol(name):
            return bias[:, BCOL[name][0]:BCOL[name][1]]

        def ccol(name):
            return const[:, CCOL[name][0]:CCOL[name][1]]

        def hcol(name):
            return half[:, HCOL[name][0]:HCOL[name][1]]

        def block_parts(words, hidden):
            v = words.bitcast(F16)
            return v[:, 0:hidden], v[:, hidden:2 * hidden], v[:, 2 * hidden:2 * hidden + P]

        def block_of(layer, e):
            return block_parts(blocks[layer][:, e * layer.block:(e + 1) * layer.block], layer.H)

        first_select = block_of(L0, 0)[2]

        def tiles(ap, n=BT):
            return ap.rearrange("p (t c) -> p t c", t=n)

        def load(dst, src, name, after=()):
            return put("sync", lambda e: e.dma_start(dst, src), after, name, 16)

        def x_view(ap, s, b):
            return ap[s * SB + b].rearrange("(t p) d -> p t d", p=P)

        x_ready = [[None] * SB for _ in range(STREAMS)]
        for b in range(SB):
            x_ready[0][b] = [load(x_res[0][:, BT * b:BT * b + BT, :], x_view(x_in, 0, b), f"x_loaded0_{b}")]
        const_loaded = load(const[:, :], const_in, "const_loaded")
        weights_loaded = load(weights[:, :], w_in, "weights_loaded")
        load(half[:, :], half_in[:, 0:HALF_KEPT], "half_loaded")
        for layer in (L0, L1):
            dst = blocks[layer][:, :].bitcast(F16).rearrange("p (e c) -> p e c", e=layer.E)[:, :, 2 * layer.H:2 * layer.H + P]
            half_loaded = load(dst, half_in[:, HALF_KEPT:HALF_KEPT + layer.E * P].rearrange("p (e c) -> p e c", c=P), "half_loaded")
        for b in range(SB):
            x_ready[1][b] = [load(x_res[1][:, BT * b:BT * b + BT, :], x_view(x_in, 1, b), f"x_loaded1_{b}")]

        zero = work.take()
        zeroed = put("gpsimd", lambda e: e.memset(zero.ap, 0.0), zero.ready, "zero_done")
        rows_free = []
        for s in range(STREAMS):
            zero_rows = rows_dram[s].rearrange("(n p a) c -> n p (a c)", p=P, a=BT)
            for n in range(MAX_TILES // BT):
                t = put("scalar", lambda e, n=n, z=zero_rows: e.dma_start(z[n], zero.ap.bitcast(F16)), [zeroed], f"rows_zeroed{s}", 16)
            rows_free.append([t])
        work.release(zero, rows_free[0][0], rows_free[1][0])

        def split_biases():
            raw = [work.take() for _ in range(3)]
            high = [work.take() for _ in range(2)]
            ready = [t for r in raw + high for t in r.ready]
            for n, r in enumerate(raw):
                loaded = load(r.ap, bias_in[:, SEQ * n:SEQ * n + SEQ], "bias_loaded", r.ready)
            pieces = []
            for lo, hi, scale in ((0, HIDDEN_BIAS_COLS, X_SCALE * W_SCALE / SEL_VALUE), (HIDDEN_BIAS_COLS, BCOLS, 1 / SEL_VALUE)):
                while lo < hi:
                    end = min(hi, (lo // SEQ + 1) * SEQ)
                    pieces.append((lo, end, scale))
                    lo = end
            clear = put("vector", lambda e: e.memset(bias[:, :], 0.0), (), "bias_step")
            for lo, hi, scale in pieces:
                src = raw[lo // SEQ].ap[:, lo % SEQ:lo % SEQ + hi - lo]
                top = high[lo // 1024].ap.bitcast(F16)[:, lo % 1024:lo % 1024 + hi - lo]
                t = put("vector", lambda e, src=src, top=top, scale=scale: e.tensor_scalar(top, src, scale, None, ALU.mult),
                        [loaded, clear] + ready, "bias_step")
                put("vector", lambda e, top=top, lo=lo, hi=hi: e.tensor_copy(bias[0:LOW_ROW, lo:hi], top[0:LOW_ROW, :]), [t], "bias_step")
                r = slice(LOW_ROW, 2 * LOW_ROW)
                t = put("vector", lambda e, src=src, top=top, lo=lo, hi=hi, scale=scale, r=r:
                        e.scalar_tensor_tensor(bias[r, lo:hi], src[r, :], scale, top[r, :], ALU.mult, ALU.subtract), [t], "bias_step")
            for r in raw + high:
                work.release(r, t)
            return t

        w1_ready = {}

        def split_w1(layer, source, e0, n):
            raw = work.take()
            loaded = load(raw.ap.rearrange("p (e h) -> p e h", e=n), source[e0:e0 + n].rearrange("e d h -> d e h"), raw.name, raw.ready)
            for i in range(n):
                high, low, _ = block_of(layer, e0 + i)
                src = raw.ap[:, i * layer.H:(i + 1) * layer.H]
                t = put("scalar", lambda e: e.activation(high, src, ACT.Copy, scale=W_SCALE), [loaded], "w1_high_done")
                done = put("vector", lambda e: e.scalar_tensor_tensor(low, src, W_SCALE, high, ALU.mult, ALU.subtract), [t, loaded], "w1_low_done")
            work.release(raw, done)
            w1_ready[layer] = [t, done]

        def layer_norm(s, b):
            sm, xn = small.take(), work.take()
            stats, mean_var, rstd = sm.ap[:, 0:24], sm.ap[:, 24:32], sm.ap[:, 32:36]
            x = x_res[s]
            for i in range(BT):
                t = put("vector", lambda e, i=i: e.bn_stats(stats[:, 6 * i:6 * i + 6], x[:, BT * b + i, :]), x_ready[s][b] + sm.ready, f"norm_stats{s}")
            for i in range(BT):
                t2 = put("vector", lambda e, i=i: e.bn_aggr(mean_var[:, 2 * i:2 * i + 2], stats[:, 6 * i:6 * i + 6]), [t], f"norm_stats{s}")
            var, sq = sm.ap[:, 36:40], sm.ap[:, 40:44]

            def step(fn):
                return put("vector", fn, [put_last[0]], f"norm_stats{s}")
            put_last = [t2]
            for fn in [lambda e: e.tensor_scalar(var, mean_var.rearrange("p (t v) -> p t v", v=2)[:, :, 1], EPS, None, ALU.add),
                       lambda e: e.tensor_scalar(rstd.bitcast(I32), var.bitcast(I32), 1, None, ALU.logical_shift_right),
                       lambda e: e.tensor_scalar(rstd.bitcast(I32), rstd.bitcast(I32), -1.0, float(RSQRT_GUESS), ALU.mult, ALU.add),
                       ] + [lambda e: e.tensor_tensor(sq, rstd, rstd, ALU.mult),
                            lambda e: e.scalar_tensor_tensor(sq, sq, -0.5, var, ALU.mult, ALU.mult),
                            lambda e: e.scalar_tensor_tensor(rstd, sq, 1.5, rstd, ALU.add, ALU.mult)] * NEWTON_STEPS:
                put_last[0] = step(fn)
            t3 = put_last[0]
            for i in range(BT):
                t4 = put("vector", lambda e, i=i: e.tensor_scalar(xn.ap[:, D * i:D * i + D], x[:, BT * b + i, :], mean_var[:, 2 * i:2 * i + 1],
                                                                 rstd[:, i:i + 1], ALU.subtract, ALU.mult), [t3] + xn.ready, f"norm_done{s}")
            small.release(sm, t4)
            return xn, t4

        def turn_batch(s, xn, xn_done):
            bk, xt = banks.take(), work.take()

            def go(e):
                for i in range(BT):
                    m = e.transpose(bk.ap[:, P * i:P * i + P], xn.ap[:, D * i:D * i + D], ccol("ident"))
                return m
            turned = put("tensor", go, [xn_done, const_loaded] + bk.ready, f"turned{s}")
            xt_done = put("scalar", lambda e: e.activation(xt.ap, bk.ap, ACT.Copy), [turned] + xt.ready, f"xt_done{s}")
            banks.release(bk, xt_done)
            return xt, xt_done, turned

        state = [dict() for _ in range(STREAMS)]

        def gate_batch(s, b, layer):
            E = layer.E
            gate_w, gate_b = (wcol("gate_w0"), wcol("gate_b0")) if layer is L0 else (wcol("gate_w1"), wcol("gate_b1"))
            st = state[s]
            if b == 0:
                st["scores"] = work.take()
                st["rows"] = []
                st["scores_done"] = []
            scores = st["scores"]
            xn, xn_done = layer_norm(s, b)
            yield 1.5
            xt, xt_done, turned = turn_batch(s, xn, xn_done)
            rows = work.take()
            parts = rows.ap.bitcast(F16).rearrange("p (t h d) -> p t h d", t=BT, h=2)
            high = put("scalar", lambda e: e.activation(parts[:, :, 0, :], tiles(xn.ap), ACT.Copy, scale=X_SCALE), [xn_done] + rows.ready, f"rows_high{s}")
            low = put("vector", lambda e: e.scalar_tensor_tensor(parts[:, :, 1, :], tiles(xn.ap), X_SCALE, parts[:, :, 0, :], ALU.mult, ALU.subtract),
                      [high], f"rows_low{s}")
            work.release(xn, turned, high, low)
            st["rows"].append((rows, [high, low]))
            yield 1.5
            bk = banks.take()

            def go(e):
                for i in range(BT):
                    m = e.matmul(bk.ap[:, E * i:E * i + E], xt.ap[:, P * i:P * i + P], gate_w, start=True, stop=True)
                return m
            scored = put("tensor", go, [xt_done, weights_loaded] + bk.ready, f"scored{s}")
            out = scores.ap[:, E * BT * b:E * BT * (b + 1)].rearrange("p (t e) -> p t e", t=BT)
            t = put("vector", lambda e: e.tensor_tensor(out, bk.ap[:, 0:BT * E].rearrange("p (t e) -> p t e", t=BT),
                                                        gate_b.unsqueeze(1).to_broadcast([P, BT, E]), ALU.add), [scored] + scores.ready, f"scores_done{s}")
            banks.release(bk, t)
            st["scores_done"].append(t)
            if layer is L1:
                xt_users = [scored]
                hidden = []
                for c in range(L1.chunks):
                    bk = banks.take()
                    made = put("tensor", lambda e, bk=bk, c=c: e.matmul(bk.ap, wcol("sw1")[:, P * c:P * c + P], xt.ap, start=True, stop=True),
                               [xt_done, weights_loaded] + bk.ready, f"shared_hidden{s}")
                    hs = work.take()
                    done = put("scalar", lambda e, bk=bk, c=c, hs=hs: e.activation(hs.ap, bk.ap, ACT.Gelu, bias=wcol("sb1")[:, c:c + 1]),
                               [made] + hs.ready, f"shared_gelu{s}")
                    banks.release(bk, done)
                    hidden.append((hs, done))
                    xt_users.append(made)
                work.release(xt, *xt_users)
                yield 3.0
                bk = banks.take()

                def go(e):
                    for i in range(BT):
                        out = bk.ap[:, D * i:D * i + D]
                        e.matmul(out, first_select, bcol("sb2"), start=True, stop=False)
                        for c in range(L1.chunks):
                            m = e.matmul(out, hidden[c][0].ap[:, P * i:P * i + P], wcol("sw2")[:, D * c:D * c + D], start=False, stop=(c == L1.chunks - 1))
                    return m
                made = put("tensor", go, [h[1] for h in hidden] + [bias_ready[0], half_loaded] + bk.ready, f"shared_out{s}")
                for hs, _ in hidden:
                    work.release(hs, made)
                xb = x_res[s][:, BT * b:BT * b + BT, :]
                t = put("vector", lambda e: e.scalar_tensor_tensor(xb, tiles(bk.ap), 0.5, xb, ALU.mult, ALU.add), [made, xn_done] + x_ready[s][b], f"x_done{s}")
                banks.release(bk, t)
                x_ready[s][b] = [t]
            else:
                work.release(xt, scored)
            yield 2.0

        def route(s, layer):
            E = layer.E
            N = E * NT
            st = state[s]
            rev = (ccol("rev0") if layer is L0 else ccol("rev1"))
            sig = f"route{s}"
            scores = st["scores"]
            sm = small.take()
            by_token = "p (t e) -> p t e"
            last = list(st["scores_done"]) + sm.ready + [const_loaded]

            def dve(fn, *more):
                t = put("vector", fn, last + list(more), sig)
                last[:] = [t]
                return t

            def over_t(ap):
                return ap.unsqueeze(2).to_broadcast([P, NT, E])

            def over_e(ap):
                return ap.unsqueeze(1).to_broadcast([P, NT, E])

            S = scores.ap[:, 0:N].rearrange(by_token, t=NT)
            if layer is L1:
                top, total = sm.ap[:, 0:NT], sm.ap[:, NT:2 * NT]
                dve(lambda e: e.tensor_reduce(top, S, AX.X, ALU.max))
                dve(lambda e: e.tensor_tensor(S, S, over_t(top), ALU.subtract))
                t = put("scalar", lambda e: e.activation(scores.ap[:, 0:N], scores.ap[:, 0:N], ACT.Exp), last, f"route_exp{s}")
                dve(lambda e: e.tensor_reduce(total, S, AX.X, ALU.add), t)
                dve(lambda e: e.reciprocal(total, total))
                dve(lambda e: e.tensor_tensor(S, S, over_t(total), ALU.mult))
            yield 3.0
            one_hot, tmp = [work.take(), work.take()], work.take()
            value = [sm.ap[:, 2 * NT:3 * NT], sm.ap[:, 3 * NT:4 * NT]]
            pick = sm.ap[:, 4 * NT:5 * NT]
            T = tmp.ap[:, 0:N].rearrange(by_token, t=NT)
            for k in range(TOP_K):
                O = one_hot[k].ap[:, 0:N].rearrange(by_token, t=NT)
                dve(lambda e, k=k: e.tensor_reduce(value[k], S, AX.X, ALU.max))
                dve(lambda e, k=k: e.tensor_tensor(T, S, over_t(value[k]), ALU.is_equal), *tmp.ready)
                dve(lambda e: e.tensor_tensor(T, T, over_e(rev), ALU.mult))
                dve(lambda e: e.tensor_reduce(pick, T, AX.X, ALU.max))
                dve(lambda e, O=O: e.tensor_tensor(O, over_e(rev), over_t(pick), ALU.is_equal), *one_hot[k].ready)
                if k == 0:
                    dve(lambda e, O=O: e.scalar_tensor_tensor(S, O, -3e38, S, ALU.mult, ALU.add))
                yield 2.5
            marks = work.take()
            mark = marks.ap.bitcast(F16)[:, 0:N]
            carry = marks.ap.bitcast(F16)[:, SEQ:SEQ + N]
            mark_v = mark.rearrange("p (e t) -> p t e", e=E)
            dve(lambda e: e.tensor_tensor(mark_v, one_hot[0].ap[:, 0:N].rearrange(by_token, t=NT), one_hot[1].ap[:, 0:N].rearrange(by_token, t=NT), ALU.add), *marks.ready)
            dve(lambda e: e.tensor_tensor_scan(tmp.ap[:, 0:N], ccol("carry")[:, 0:N], mark, 0.0, ALU.mult, ALU.add))
            dve(lambda e: e.tensor_tensor(carry, tmp.ap[:, 0:N], mark, ALU.subtract))
            lastc = marks.ap.bitcast(F16)[:, SEQ - 2 * L0.E:SEQ - 2 * L0.E + E]
            counted = dve(lambda e: e.tensor_copy(lastc, tmp.ap[:, 0:N].rearrange("p (e t) -> p e t", e=E)[:, :, NT - 1]))
            bk = banks.take()

            def go(e):
                e.matmul(bk.ap[:, 0:N], hcol("before"), mark, start=True, stop=False)
                e.matmul(bk.ap[:, 0:N], hcol("ones"), carry, start=False, stop=True)
                return e.matmul(bk.ap[:, N:N + E], hcol("ones"), lastc, start=True, stop=True)
            ranked = put("tensor", go, [counted, half_loaded] + bk.ready, f"ranked{s}")
            yield 2.0
            sm2 = small.take()
            need_i = sm2.ap[:, 0:E].bitcast(I32)
            need, end, base = sm2.ap[:, E:2 * E], sm2.ap[:, 2 * E:3 * E], sm2.ap[:, 3 * E:4 * E]
            dve(lambda e: e.tensor_scalar(need_i, bk.ap[:, N:N + E], float(P - 1), None, ALU.add), ranked, *sm2.ready)
            dve(lambda e: e.tensor_scalar(need_i, need_i, P.bit_length() - 1, None, ALU.arith_shift_right))
            dve(lambda e: e.tensor_copy(need, need_i))
            dve(lambda e: e.tensor_tensor_scan(end, hcol("ones")[:, 0:E], need, 0.0, ALU.mult, ALU.add))
            dve(lambda e: e.tensor_tensor(base, end, need, ALU.subtract))
            dve(lambda e: e.tensor_scalar(base, base, float(P), None, ALU.mult))
            R = tmp.ap[:, 0:N].rearrange("p (e t) -> p e t", e=E)
            dve(lambda e: e.tensor_tensor(R, bk.ap[:, 0:N].rearrange("p (e t) -> p e t", e=E), base.unsqueeze(2).to_broadcast([P, E, NT]), ALU.add))
            banks.release(bk, last[0])
            Rt = tmp.ap[:, 0:N].rearrange("p (e t) -> p t e", e=E)
            for k in range(TOP_K):
                O = one_hot[k].ap[:, 0:N].rearrange(by_token, t=NT)
                dve(lambda e, O=O: e.tensor_tensor(O, O, Rt, ALU.mult))
                dve(lambda e, O=O: e.tensor_reduce(pick, O, AX.X, ALU.add))
                indexed = dve(lambda e, k=k: e.tensor_copy(slot_index[s][:, k, :], pick), *st.get("index_free", []))
            yield 3.0
            scattered = []
            for b in range(SB):
                rows, made = st["rows"][b]
                for i in range(BT):
                    for k in range(TOP_K):
                        src = rows.ap.bitcast(F16)[:, 2 * D * i:2 * D * i + 2 * D]
                        at = slot_index[s][:, k, BT * b + i:BT * b + i + 1]
                        t = put("gpsimd", lambda e, src=src, at=at: e.indirect_dma_start(
                            rows_dram[s], bass.IndirectOffsetOnAxis(ap=at, axis=0), src, None), made + [indexed] + rows_free[s], rows.name + "_scattered", 16)
                work.release(rows, t)
                scattered.append(t)
            st["scattered"] = scattered
            ej = sm.ap[:, 0:1]
            dve(lambda e: e.tensor_scalar(need, end, ccol("iota"), None, ALU.is_le))
            dve(lambda e: e.tensor_reduce(ej, need, AX.X, ALU.add))
            named = dve(lambda e: e.tensor_scalar(ej, ej, float(E - 1), None, ALU.min))
            bk = banks.take()
            turned = put("tensor", lambda e: e.matmul(bk.ap[0:1, 0:P], ej, ccol("ident"), start=True, stop=True), [named] + bk.ready, f"ranked{s}")
            dve(lambda e: e.tensor_scalar(tile_expert[s][0:1, 0, 0:layer.tiles], bk.ap[0:1, 0:layer.tiles], float(layer.block), None, ALU.mult), turned, *st.get("expert_free", []))
            dve(lambda e: e.tensor_scalar(tile_expert[s][0:1, 1, 0:layer.tiles], bk.ap[0:1, 0:layer.tiles], 1.0, None, ALU.mult))
            banks.release(bk, last[0])
            st["experts_named"] = last[0]
            if layer is L0:
                gap = sm.ap[:, NT:2 * NT]
                t = dve(lambda e: e.tensor_tensor(gap, value[1], value[0], ALU.subtract))
                t = put("scalar", lambda e: e.activation(gap, gap, ACT.Exp), [t], f"route_exp{s}")
                dve(lambda e: e.tensor_scalar(pick, gap, 1.0, None, ALU.add), t)
                dve(lambda e: e.reciprocal(pick, pick))
                dve(lambda e: e.tensor_scalar(share[s][:, 0, :], pick, 0.5, None, ALU.mult))
                dve(lambda e: e.tensor_tensor(share[s][:, 1, :], share[s][:, 0, :], gap, ALU.mult))
            else:
                for k in range(TOP_K):
                    dve(lambda e, k=k: e.tensor_scalar(share[s][:, k, :], value[k], 0.5, None, ALU.mult))
            st["shared_out"] = last[0]
            for sl in one_hot + [tmp, marks, scores]:
                work.release(sl, last[0])
            small.release(sm, last[0])
            small.release(sm2, last[0])
            yield 25.0

        def experts(s, layer):
            H, C = layer.H, layer.chunks
            st = state[s]
            groups = layer.tiles // BT
            w2_dram = (w2_0 if layer is L0 else w2_1).rearrange("e (c p) d -> p e c d", p=P)
            b1, b2 = (bcol("b1_0"), bcol("b2_0")) if layer is L0 else (bcol("b1_1"), bcol("b2_1"))
            turned_rows = {}
            rows_read = []
            block_at, w2_at = {}, {}

            def read_tile_experts(g):
                for row, engine, values, top in ((0, VECTOR, block_at, (layer.E - 1) * layer.block), (1, SYNC, w2_at, layer.E - 1)):
                    put(engine, lambda e: None, [st["experts_named"]])
                    _, regs = nc.values_load_multi_w_load_instructions(
                        tile_expert[s][0:1, row, BT * g:BT * g + BT], engines=[ENGINE_TYPE[engine]], min_val=0, max_val=top, skip_runtime_bounds_check_because="the counts keep them in range")
                    for i, r in enumerate(regs):
                        values[BT * g + i] = r

            def bring_weights(unit):
                blk, second = block_slots[s].take(), work.take()
                for j in range(layer.unit):
                    tile = unit * layer.unit + j
                    dst = blk.ap[:, j * layer.block:(j + 1) * layer.block]
                    copied = put("vector", lambda e: e.tensor_copy(dst, blocks[layer][:, bass.ds(block_at[tile], layer.block)]),
                                 w1_ready[layer] + [half_loaded] + blk.ready, f"block_copied{s}")
                    dst2 = second.ap[:, j * H:(j + 1) * H].rearrange("p (o c d) -> p o c d", o=1, c=C)
                    landed = load(dst2, w2_dram[:, bass.ds(w2_at[tile], 1)], second.name, second.ready)
                return blk, copied, second, landed

            def fetch(g):
                rows = work.take()
                src = rows_dram[s][g * BT * P:(g + 1) * BT * P].rearrange("(t p) c -> p t c", p=P)
                t = load(rows.ap.bitcast(F16).rearrange("p (t c) -> p t c", t=BT), src, rows.name, st["scattered"] + rows.ready)
                rows_read.append(t)
                return rows, t

            def turn(g, rows, loaded):
                bk, xt = turn_banks.take(), work.take()
                R = rows.ap.bitcast(F16).rearrange("p (n d) -> p n d", d=D)

                def go(e):
                    for n in range(2 * BT):
                        m = e.transpose(bk.ap[:, P * n:P * n + P], R[:, n, :], hcol("ident"))
                    return m
                turned = put("tensor", go, [loaded, half_loaded] + bk.ready, f"rows_turned{s}")
                work.release(rows, turned)
                done = put("scalar", lambda e: e.activation(xt.ap.bitcast(F16), bk.ap, ACT.Copy), [turned] + xt.ready, f"rows_xt{s}")
                turn_banks.release(bk, done)
                turned_rows[g] = (xt, done)

            fetched = [fetch(0), fetch(1)]
            read_tile_experts(0)
            brought = [bring_weights(0), bring_weights(1)]
            units = layer.tiles // layer.unit
            turn(0, *fetched[0])
            pending = None
            out_bank = None
            users = []
            y_stored = None
            for unit in range(units):
                first = unit * layer.unit
                g = first // BT
                if first % BT == 0:
                    if g + 2 < groups:
                        fetched.append(fetch(g + 2))
                xt, xt_done = turned_rows[g]
                hb, hid = hidden_banks.take(), work.take()

                blk, copied, second, landed = brought[unit]

                def layer1(e):
                    X = xt.ap.bitcast(F16).rearrange("p (t h n) -> p t h n", t=BT, h=2)
                    for j in range(layer.unit):
                        xh, xl = X[:, (first + j) % BT, 0, :], X[:, (first + j) % BT, 1, :]
                        high, low, select = block_parts(blk.ap[:, j * layer.block:(j + 1) * layer.block], H)
                        for c in range(C):
                            out = hb.ap[:, j * H + c * P:j * H + c * P + P]
                            e.matmul(out, b1[:, c * P:c * P + P], select, start=True, stop=False)
                            e.matmul(out, high[:, c * P:c * P + P], xh, start=False, stop=False)
                            e.matmul(out, high[:, c * P:c * P + P], xl, start=False, stop=False)
                            m = e.matmul(out, low[:, c * P:c * P + P], xh, start=False, stop=True)
                    return m
                made = put("tensor", layer1, [xt_done, copied, bias_ready[0]] + hb.ready, f"hidden_made{s}")
                if (first + layer.unit) % BT == 0:
                    work.release(xt, made)
                gelu = put("scalar", lambda e, hb=hb, hid=hid: e.activation(hid.ap, hb.ap, ACT.Gelu, scale=1 / (X_SCALE * W_SCALE)),
                           [made] + hid.ready, f"hidden_gelu{s}")
                hidden_banks.release(hb, gelu)
                if first % BT == BT // 2 and g + 1 < groups:
                    turn(g + 1, *fetched[g + 1])
                ripe = ([pending] if pending else []) + ([(first, hid, gelu, brought[unit])] if unit == units - 1 else [])
                for first2, hid2, gelu2, (blk2, copied2, second2, landed2) in ripe:
                    if first2 % BT == 0:
                        out_bank = out_banks.take()

                    def layer2(e):
                        for j in range(layer.unit):
                            out = out_bank.ap[:, D * ((first2 + j) % BT):D * ((first2 + j) % BT) + D]
                            select = block_parts(blk2.ap[:, j * layer.block:(j + 1) * layer.block], H)[2]
                            e.matmul(out, select, b2, start=True, stop=False)
                            for c in range(C):
                                at = slice(j * H + c * P, j * H + c * P + P)
                                m = e.matmul(out, hid2.ap[:, at], second2.ap[:, at], start=False, stop=(c == C - 1))
                        return m
                    done = put("tensor", layer2, [gelu2, landed2, copied2] + out_bank.ready, f"expert_out{s}")
                    block_slots[s].release(blk2, done)
                    work.release(second2, done)
                    work.release(hid2, done)
                    if (first2 + layer.unit) % BT == 0:
                        g2 = first2 // BT
                        y = work.take()
                        copied = put("vector", lambda e, ob=out_bank, y=y: e.tensor_copy(y.ap, ob.ap), [done] + y.ready, f"y_copied{s}")
                        out_banks.release(out_bank, copied)
                        dst = y_dram[s][g2 * BT * P:(g2 + 1) * BT * P].rearrange("(t p) d -> p t d", p=P)
                        y_stored = put("sync", lambda e, dst=dst, y=y: e.dma_start(dst, tiles(y.ap)), [copied] + st.get("y_free", []), y.name, 16)
                        work.release(y, y_stored)
                        users.append(y_stored)
                pending = (first, hid, gelu, brought[unit])
                if unit + 2 < units:
                    if (unit + 2) * layer.unit % BT == 0:
                        read_tile_experts((unit + 2) * layer.unit // BT)
                    brought.append(bring_weights(unit + 2))
                yield 2.0
            rows_free[s] = rows_read
            st["expert_free"] = [copied, landed]
            st["y_stored"] = users

        def combine_batch(s, b):
            st = state[s]
            x = x_res[s]
            if b == 0:
                st["y_free"], st["index_free"] = [], []
            for pair in range(BT // 2):
                got = work.take()
                where = []
                for i in range(2):
                    for k in range(TOP_K):
                        t = BT * b + 2 * pair + i
                        col = D * (2 * i + k)
                        where.append((t, k, col))
                        at = slot_index[s][:, k, t:t + 1]
                        landed = put("gpsimd", lambda e, got=got, col=col, at=at: e.indirect_dma_start(
                            got.ap[:, col:col + D], None, y_dram[s], bass.IndirectOffsetOnAxis(ap=at, axis=0)),
                            st["y_stored"] + got.ready, got.name + "_gathered", 16)
                st["y_free"] = st["y_free"] + [landed]
                st["index_free"] = st["index_free"] + [landed]
                for t, k, col in where:
                    done = put("vector", lambda e, t=t, k=k, col=col, got=got: e.scalar_tensor_tensor(
                        x[:, t, :], got.ap[:, col:col + D], share[s][:, k, t:t + 1], x[:, t, :], ALU.mult, ALU.add),
                        [landed, st["shared_out"]] + x_ready[s][b], f"x_done{s}")
                    x_ready[s][b] = [done]
                work.release(got, done)
                yield 5.0

        def linear_attention(s, b):
            xn, xn_done = layer_norm(s, b)
            yield 1.5
            xt, xt_done, turned = turn_batch(s, xn, xn_done)
            work.release(xn, turned)
            yield 1.5
            first = {}
            for name, mat, bi in (("q", "q1", "q_b1"), ("k", "k1", "k_b1"), ("v", "v", "v_b"), ("g", "g", "g_b")):
                bk, out = banks.take(), work.take()
                made = put("tensor", lambda e, bk=bk, mat=mat: e.matmul(bk.ap, wcol(mat), xt.ap, start=True, stop=True),
                           [xt_done, weights_loaded] + bk.ready, f"attn_made{s}")
                done = put("scalar", lambda e, bk=bk, out=out, bi=bi: e.activation(out.ap, bk.ap, ACT.Gelu, bias=wcol(bi)), [made] + out.ready, f"attn_gelu{s}")
                banks.release(bk, done)
                first[name] = (out, done)
                if name == "k":
                    yield 1.7
            work.release(xt, made)
            yield 1.7
            second = {}
            zs = []
            for name, mat, bi in (("q", "q2", "q_b2"), ("k", "k2", "k_b2")):
                hid, hid_done = first[name]
                bk, z, mag = banks.take(), work.take(), work.take()

                def go(e, bk=bk, hid=hid, mat=mat, bi=bi):
                    for i in range(BT):
                        out = bk.ap[:, D * i:D * i + D]
                        e.matmul(out, first_select, bcol(bi), start=True, stop=False)
                        m = e.matmul(out, hid.ap[:, P * i:P * i + P], wcol(mat), start=False, stop=True)
                    return m
                made = put("tensor", go, [hid_done, bias_ready[0], half_loaded] + bk.ready, f"attn_made{s}")
                work.release(hid, made)
                pos = put("vector", lambda e, bk=bk, z=z: e.tensor_scalar(z.ap, bk.ap, 0.0, None, ALU.max), [made] + z.ready, f"attn_dve{s}")
                size = put("vector", lambda e, bk=bk, z=z, mag=mag: e.scalar_tensor_tensor(mag.ap, z.ap, -2.0, bk.ap, ALU.mult, ALU.add),
                           [pos] + mag.ready, f"attn_dve{s}")
                banks.release(bk, size)
                zs.append((name, z, mag, size))
            yield 1.7
            exps = []
            for name, z, mag, size in zs:
                exps.append(put("scalar", lambda e, mag=mag: e.activation(mag.ap, mag.ap, ACT.Exp), [size], f"attn_exp{s}"))
            for (name, z, mag, size), ex in zip(zs, exps):
                ln = put("scalar", lambda e, mag=mag: e.activation(mag.ap, mag.ap, ACT.Ln, bias=ccol("one")), [ex, const_loaded], f"attn_exp{s}")
                done = put("vector", lambda e, z=z, mag=mag: e.tensor_tensor(z.ap, z.ap, mag.ap, ALU.add), [ln], f"attn_dve{s}")
                work.release(mag, done)
                second[name] = (z, done)
            yield 3.0
            (qs, q_done), (ks, k_done) = second["q"], second["k"]
            bk, sm, at_ = banks.take(), small.take(), work.take()

            def go(e):
                for i in range(BT):
                    m = e.matmul(bk.ap[:, 0:D], ks.ap[:, D * i:D * i + D], qs.ap[:, D * i:D * i + D], start=(i == 0), stop=(i == BT - 1))
                return m
            made = put("tensor", go, [q_done, k_done] + bk.ready, f"attn_made{s}")
            work.release(qs, made)
            work.release(ks, made)
            heads = at_.ap[:, 0:D]
            masked = put("vector", lambda e: e.tensor_tensor(heads, bk.ap[:, 0:D], ccol("heads"), ALU.mult), [made, const_loaded] + at_.ready, f"attn_dve{s}")
            banks.release(bk, masked)
            yield 1.0
            (vt, v_done), (gt, g_done) = first["v"], first["g"]
            bk, bk2 = banks.take(), banks.take()
            summed = put("tensor", lambda e: e.matmul(bk2.ap[:, 0:1], heads, ccol("one"), start=True, stop=True), [masked] + bk2.ready, f"attn_made{s}")
            made = put("tensor", lambda e: e.matmul(bk.ap, heads, vt.ap, start=True, stop=True), [v_done] + bk.ready, f"attn_made{s}")
            z1, z2 = sm.ap[:, 0:1], sm.ap[:, 1:2]
            t = put("vector", lambda e: e.tensor_scalar(z1, bk2.ap[:, 0:1], float(D), None, ALU.add), [summed] + sm.ready, f"attn_dve{s}")
            banks.release(bk2, t)
            zinv = put("vector", lambda e: e.reciprocal(z2, z1), [t], f"attn_dve{s}")
            t = put("vector", lambda e: e.tensor_tensor(vt.ap, bk.ap, vt.ap, ALU.add), [made], f"attn_dve{s}")
            banks.release(bk, t)
            work.release(at_, made)
            o = work.take()
            o_view = o.ap.rearrange("p (c a) -> p a c", a=SEQ // HEADS)
            gated = put("vector", lambda e: e.scalar_tensor_tensor(o_view, vt.ap.rearrange("p (a c) -> p a c", c=HEADS), z2,
                                                                   gt.ap.rearrange("p (a c) -> p a c", c=HEADS), ALU.mult, ALU.mult),
                        [t, zinv, g_done] + o.ready, f"attn_dve{s}")
            small.release(sm, gated)
            work.release(vt, gated)
            work.release(gt, gated)
            hd = heads_dram[s * SB + b]
            stored = put("sync", lambda e: e.dma_start(hd, o.ap), [gated], o.name, 16)
            work.release(o, stored)
            m = work.take()
            src = hd.rearrange("(h n) (c a) -> c n h a", n=HEAD_DIM, c=HEADS)
            per_load = 1
            for c in range(HEADS):
                dst = m.ap[HEAD_DIM * c:HEAD_DIM * c + HEAD_DIM, :].rearrange("n (h a) -> n h a", h=HEADS)
                landed = put("sync", lambda e, c=c, dst=dst: e.dma_start(dst, src[c]), [stored] + m.ready, m.name, 16)
            yield 8.0
            bk = banks.take()

            def go2(e):
                for i in range(BT):
                    out = bk.ap[:, D * i:D * i + D]
                    e.matmul(out, first_select, bcol("p_b"), start=True, stop=False)
                    mm = e.matmul(out, m.ap[:, P * i:P * i + P], wcol("p"), start=False, stop=True)
                return mm
            made = put("tensor", go2, [landed] + bk.ready, f"attn_made{s}")
            work.release(m, made)
            xb = x_res[s][:, BT * b:BT * b + BT, :]
            t = put("vector", lambda e: e.tensor_tensor(xb, tiles(bk.ap), xb, ALU.add), [made, xn_done] + x_ready[s][b], f"x_done{s}")
            banks.release(bk, t)
            x_ready[s][b] = [t]
            yield 1.0

        def causal_attention(s, b):
            xn, xn_done = layer_norm(s, b)
            yield 1.5
            xt, xt_done, turned = turn_batch(s, xn, xn_done)
            work.release(xn, turned)
            yield 1.5
            roped = []
            for mat in ("wq", "wk"):
                parts = []
                for m_name, table in ((mat, "cos"), (mat + "_swap", "sin")):
                    bk, out = banks.take(), work.take()
                    made = put("tensor", lambda e, bk=bk, m_name=m_name: e.matmul(bk.ap, wcol(m_name), xt.ap, start=True, stop=True),
                               [xt_done, weights_loaded] + bk.ready, f"attn_made{s}")
                    done = put("vector", lambda e, bk=bk, out=out, table=table: e.tensor_tensor(out.ap, bk.ap, ccol(table), ALU.mult),
                               [made, const_loaded] + out.ready, f"attn_dve{s}")
                    banks.release(bk, done)
                    parts.append((out, done))
                (a, a_done), (c, c_done) = parts
                done = put("gpsimd", lambda e, a=a, c=c: e.tensor_tensor(a.ap, a.ap, c.ap, ALU.add), [a_done, c_done], f"roped{s}")
                work.release(c, done)
                roped.append((a, done))
                yield 2.0
            bk, v = banks.take(), work.take()

            def go(e):
                for i in range(BT):
                    m = e.matmul(bk.ap[:, D * i:D * i + D], xt.ap[:, P * i:P * i + P], wcol("wv"), start=True, stop=True)
                return m
            made = put("tensor", go, [xt_done] + bk.ready, f"attn_made{s}")
            work.release(xt, made)
            v_done = put("scalar", lambda e: e.activation(v.ap, bk.ap, ACT.Copy), [made] + v.ready, f"attn_copy{s}")
            banks.release(bk, v_done)
            yield 1.0
            (qt, q_done), (kt, k_done) = roped
            sm = small.take()
            for i in range(BT):
                n = P * (i + 1)
                top, neg, total, inv = (sm.ap[:, 4 * i + j:4 * i + j + 1] for j in range(4))
                bk, pr = banks.take(), work.take()
                made = put("tensor", lambda e, bk=bk, i=i, n=n: e.matmul(bk.ap[:, 0:n], qt.ap[:, P * i:P * i + P], kt.ap[:, 0:n], start=True, stop=True),
                           [q_done, k_done] + bk.ready, f"attn_made{s}")
                diag = bk.ap[:, P * i:n]
                t = put("vector", lambda e, diag=diag: e.tensor_tensor(diag, diag, ccol("causal"), ALU.add), [made], f"attn_dve{s}")
                t = put("vector", lambda e, bk=bk, n=n, top=top: e.tensor_reduce(top, bk.ap[:, 0:n], AX.X, ALU.max), [t] + sm.ready, f"attn_dve{s}")
                t = put("vector", lambda e, top=top, neg=neg: e.tensor_scalar(neg, top, -ATTN_SCALE, None, ALU.mult), [t], f"attn_dve{s}")
                ex = put("scalar", lambda e, bk=bk, pr=pr, n=n, neg=neg, total=total: e.activation(
                    pr.ap[:, 0:n], bk.ap[:, 0:n], ACT.Exp, bias=neg, scale=ATTN_SCALE, accum_out=total), [t] + pr.ready, f"attn_exp{s}")
                banks.release(bk, ex)
                yield 1.5
                bk, prt = banks.take(), work.take()

                def go(e, bk=bk, pr=pr, i=i):
                    for j in range(i + 1):
                        m = e.transpose(bk.ap[:, P * j:P * j + P], pr.ap[:, P * j:P * j + P], ccol("ident"))
                    return m
                turned = put("tensor", go, [ex] + bk.ready, f"attn_made{s}")
                work.release(pr, turned)
                copied = put("scalar", lambda e, bk=bk, prt=prt, n=n: e.activation(prt.ap[:, 0:n], bk.ap[:, 0:n], ACT.Copy), [turned] + prt.ready, f"attn_copy{s}")
                banks.release(bk, copied)
                r = put("vector", lambda e, total=total, inv=inv: e.reciprocal(inv, total), [ex], f"attn_dve{s}")
                yield 1.5
                bk = banks.take()

                def go(e, bk=bk, prt=prt, i=i):
                    for j in range(i + 1):
                        m = e.matmul(bk.ap[:, 0:D], prt.ap[:, P * j:P * j + P], v.ap[:, D * j:D * j + D], start=(j == 0), stop=(j == i))
                    return m
                made = put("tensor", go, [copied, v_done] + bk.ready, f"attn_made{s}")
                work.release(prt, made)
                xi = x_res[s][:, BT * b + i, :]
                t = put("vector", lambda e, bk=bk, xi=xi, inv=inv: e.scalar_tensor_tensor(xi, bk.ap[:, 0:D], inv, xi, ALU.mult, ALU.add),
                        [made, r, xn_done] + x_ready[s][b], f"x_done{s}")
                banks.release(bk, t)
                yield 0.5
            x_ready[s][b] = [t]
            small.release(sm, t)
            for sl in (qt, kt, v):
                work.release(sl, made)

        bias_ready = [None]

        def stream(s):
            for b in range(SB):
                yield from gate_batch(s, b, L0)
                if s == 0:
                    for e in range(b * L0.E // SB, (b + 1) * L0.E // SB):
                        split_w1(L0, w1_0, e, 1)
                    if b == 0:
                        bias_ready[0] = split_biases()
                    yield 4.0
            yield from route(s, L0)
            yield from experts(s, L0)
            if s == 0:
                for e in range(0, L1.E, L1.unit):
                    split_w1(L1, w1_1, e, L1.unit)
            for b in range(SB):
                yield from combine_batch(s, b)
                yield from linear_attention(s, b)
                yield from gate_batch(s, b, L0)
            yield from route(s, L0)
            yield from experts(s, L0)
            for b in range(SB):
                yield from combine_batch(s, b)
                yield from gate_batch(s, b, L1)
            yield from route(s, L1)
            yield from experts(s, L1)
            for b in range(SB):
                yield from combine_batch(s, b)
                yield from causal_attention(s, b)
                yield from gate_batch(s, b, L1)
            yield from route(s, L1)
            yield from experts(s, L1)
            for b in range(SB):
                yield from combine_batch(s, b)
                put("sync", lambda e, b=b: e.dma_start(x_view(x_out, s, b), x_res[s][:, BT * b:BT * b + BT, :]), x_ready[s][b], "x_stored", 16)

        running = [[0.0, stream(0)], [70.0, stream(1)]]
        while running:
            turn = min(running, key=lambda r: r[0])
            try:
                turn[0] += next(turn[1])
            except StopIteration:
                running.remove(turn)

        written = [Token(name, q.count[name]) for name in q.sems if name.startswith("work") or name in ("x_stored", "rows_zeroed0", "rows_zeroed1")]
        put("sync", lambda e: None, written)


def constants():
    f = np.float32
    c = np.zeros((P, CCOLS), f)

    def put(name, value):
        c[:, CCOL[name][0]:CCOL[name][1]] = value
    r = np.arange(P)
    put("ident", np.eye(P, dtype=f))
    put("heads", (r[:, None] // HEAD_DIM == r[None, :] // HEAD_DIM) * f(HEAD_SCALE))
    put("causal", np.where(r[None, :] > r[:, None], f(-1e30), f(0)))
    inv_freq = f(1) / f(10000.0) ** (np.arange(0, D, 2, dtype=f) / f(D))
    freqs = np.arange(SEQ, dtype=f)[:, None] * inv_freq
    put("cos", np.repeat(np.cos(freqs), 2, axis=-1).T)
    put("sin", np.repeat(np.sin(freqs), 2, axis=-1).T * np.where(r % 2 == 0, f(-1), f(1))[:, None])
    put("carry", np.tile((np.arange(NT) > 0).astype(f), L0.E)[None, :])
    put("rev0", (L0.E - np.arange(L0.E)).astype(f)[None, :])
    put("rev1", (L1.E - np.arange(L1.E)).astype(f)[None, :])
    put("iota", r[:, None])
    put("one", 1)
    h = np.zeros((P, HCOLS), np.float16)
    h[:, HCOL["ident"][0]:HCOL["ident"][1]] = np.eye(P)
    h[:, HCOL["before"][0]:HCOL["before"][1]] = r[:, None] < r[None, :]
    h[:, HCOL["ones"][0]:HCOL["ones"][1]] = 1
    sel = np.zeros((P, L0.E, P), np.float16)
    for e in range(L0.E):
        sel[e, e, :] = sel[LOW_ROW + e, e, :] = SEL_VALUE
    h[:, HCOL["select"][0]:HCOL["select"][1]] = sel.reshape(P, -1)
    return c, h


def kernel(**inputs):
    import concourse.bacc as bacc
    from concourse.bass_utils import run_bass_kernel_spmd

    a = {k: np.asarray(v) for k, v in inputs.items()}
    swap = np.arange(D) ^ 1
    mats = {"q1": a["L0_attn_q_w1"], "k1": a["L0_attn_k_w1"], "v": a["L0_attn_v_w"], "g": a["L0_attn_g_w"],
            "q2": a["L0_attn_q_w2"], "k2": a["L0_attn_k_w2"], "p": a["L0_attn_p_w"],
            "wq": a["L1_attn_wq"], "wq_swap": a["L1_attn_wq"][swap], "wk": a["L1_attn_wk"], "wk_swap": a["L1_attn_wk"][swap],
            "wv": a["L1_attn_wv"]}
    w = np.zeros((P, WCOLS), np.float32)
    for name, m in mats.items():
        w[:, WCOL[name][0]:WCOL[name][1]] = m.T
    for name, m in (("gate_w0", a["L0_ffn_gate_w"]), ("gate_w1", a["L1_ffn_router_w"]),
                    ("gate_b0", a["L0_ffn_gate_b"][None, :]), ("gate_b1", a["L1_ffn_router_b"][None, :]), ("sw1", a["L1_ffn_sw1"]),
                    ("sw2", a["L1_ffn_sw2"].reshape(L1.chunks, P, D).transpose(1, 0, 2).reshape(P, -1)),
                    ("q_b1", a["L0_attn_q_b1"][:, None]), ("k_b1", a["L0_attn_k_b1"][:, None]), ("v_b", a["L0_attn_v_b"][:, None]),
                    ("g_b", a["L0_attn_g_b"][:, None]), ("sb1", a["L1_ffn_sb1"].reshape(L1.chunks, P).T)):
        w[:, WCOL[name][0]:WCOL[name][1]] = m
    rows = np.zeros((P, BCOLS), np.float32)
    for name, m in (("b1_0", a["L0_ffn_b1"]), ("b1_1", a["L1_ffn_rb1"]), ("b2_0", a["L0_ffn_b2"]), ("b2_1", a["L1_ffn_rb2"]),
                    ("q_b2", a["L0_attn_q_b2"][None, :]), ("k_b2", a["L0_attn_k_b2"][None, :]), ("p_b", a["L0_attn_p_b"][None, :]),
                    ("sb2", a["L1_ffn_sb2"][None, :])):
        for at in (0, LOW_ROW):
            rows[at:at + m.shape[0], BCOL[name][0]:BCOL[name][1]] = m
    c, h = constants()
    arrays = {"x": a["L0_attn_x"], "w": w, "bias_rows": rows, "const": c, "half": h, "w1_0": a["L0_ffn_w1"], "w2_0": a["L0_ffn_w2"],
              "w1_1": a["L1_ffn_rw1"], "w2_1": a["L1_ffn_rw2"]}
    arrays = {f"in_{k}_dram": np.ascontiguousarray(v) for k, v in arrays.items()}
    nc = bacc.Bacc("TRN2", target_bir_lowering=False, num_devices=1)
    args = [nc.dram_tensor(k, v.shape, mybir.dt.from_np(v.dtype), kind="ExternalInput").ap() for k, v in arrays.items()]
    args.append(nc.dram_tensor("out_0_dram", (BATCHES, SEQ, D), F32, kind="ExternalOutput").ap())
    macaron_program(nc, *args)
    r = run_bass_kernel_spmd(nc, [arrays], core_ids=[0])
    return r.results[0]["out_0_dram"]
```

```python
from contextlib import ExitStack

import concourse.bass as bass
import numpy as np
from concourse import mybir

F32 = mybir.dt.float32
F16 = mybir.dt.float16
I32 = mybir.dt.int32
ALU = mybir.AluOpType
ACT = mybir.ActivationFunctionType
AX = mybir.AxisListType
VECTOR, SYNC = "vector", "sync"
ENGINE_TYPE = {VECTOR: mybir.EngineType.DVE, SYNC: mybir.EngineType.SP}

P = 128
D = 128
BATCHES, SEQ = 8, 512
STREAMS = 2
SB = BATCHES // STREAMS
BT = SEQ // P
NT = SB * BT
TOP_K = 2
EPS = 1e-5
RSQRT_GUESS = 0x5F3759DF
NEWTON_STEPS = 3

HEADS = 16
HEAD_DIM = D // HEADS
HEAD_SCALE = HEAD_DIM ** -0.5
ATTN_SCALE = D ** -0.5

X_SCALE = 32.0
W_SCALE = 32.0
SEL_VALUE = 4.0
LOW_ROW = 32


PASS_TIME = 0.0535
GATHER_TIME = 1.04
BATCH_STAGGER = 4.0
STREAM_DELAY = 40.0
MIN_FREE = 16


class Layer:

    def __init__(self, name, experts, hidden):
        self.name, self.E, self.H = name, experts, hidden
        self.chunks = hidden // P
        pairs = NT * P * TOP_K
        bound = (pairs - experts) // P + experts
        self.tiles = -(-bound // BT) * BT
        self.unit = SEQ // hidden
        self.block = hidden + P // 2


L0 = Layer("l0", 24, 512)
L1 = Layer("l1", 8, 256)
MAX_TILES = max(L0.tiles, L1.tiles)

MATS = ["q1", "k1", "v", "g", "q2", "k2", "p", "wq", "wq_swap", "wk", "wk_swap", "wv"]


def columns(widths):
    at, out = 0, {}
    for name, n in widths:
        out[name] = (at, at + n)
        at += n
    return out, at


WCOL, WCOLS = columns([(m, D) for m in MATS] + [
    ("gate_w0", L0.E), ("gate_w1", L1.E), ("gate_b0", L0.E), ("gate_b1", L1.E),
    ("sw1", L1.H), ("sw2", L1.chunks * D), ("q_b1", 1), ("k_b1", 1), ("v_b", 1), ("g_b", 1), ("sb1", L1.chunks)])
BCOL, BCOLS = columns([("b1_0", L0.H), ("b1_1", L1.H), ("b2_0", D), ("b2_1", D),
                       ("q_b2", D), ("k_b2", D), ("p_b", D), ("sb2", D)])
HIDDEN_BIAS_COLS = L0.H + L1.H
CCOL, CCOLS = columns([("ident", P), ("heads", D), ("causal", P), ("cos", SEQ), ("sin", SEQ),
                       ("carry", L0.E * NT), ("rev0", L0.E), ("rev1", L1.E), ("iota", 1), ("one", 1)])
HCOL, HCOLS = columns([("ident", P), ("before", P), ("ones", P), ("select", L0.E * P)])
HALF_KEPT = HCOL["select"][0]


class Token:

    def __init__(self, sem, value):
        self.sem, self.value = sem, value


class Queues:

    def __init__(self, nc, ctx):
        self.nc, self.ctx = nc, ctx
        self.sems, self.count = {}, {}
        self.engines = {"tensor": nc.tensor, "vector": nc.vector, "scalar": nc.scalar, "gpsimd": nc.gpsimd, "sync": nc.sync}
        self.waited = {e: {} for e in self.engines}

    def put(self, engine, work, after, signal=None, by=1):
        waits = []
        seen = self.waited[engine]
        best = {}
        for t in after:
            best[t.sem] = max(best.get(t.sem, 0), t.value)
        for name, value in best.items():
            if seen.get(name, 0) < value:
                seen[name] = value
                waits.append((name, value))
        if signal is not None:
            if signal not in self.sems:
                self.sems[signal] = self.ctx.enter_context(self.nc.semaphore(signal))
                self.count[signal] = 0
            self.count[signal] += by
        eng = self.engines[engine]
        for name, value in waits:
            eng.wait_ge(self.sems[name], value)
        last = work(eng)
        if signal is not None:
            last.then_inc(self.sems[signal], by)
        return Token(signal, self.count[signal]) if signal is not None else None


class Slot:
    def __init__(self, ap, name):
        self.ap, self.name, self.ready = ap, name, []


class Slots:

    def __init__(self, aps, name):
        self.free = [Slot(ap, f"{name}{i}") for i, ap in enumerate(aps)]

    def take(self):
        return self.free.pop(0)

    def release(self, slot, *tokens):
        slot.ready = list(tokens)
        self.free.append(slot)


class Filler:
    pass


class Urgent:
    pass


class Part:
    def __init__(self, steps, ready, parent=None):
        self.steps, self.ready, self.parent = steps, ready, parent
        self.filler, self.children, self.fresh = False, 0, parent is not None


def interleave(streams, work):
    now = 0.0
    parts = [Part(steps, 0.0) for steps in streams]
    while parts:
        able = [p for p in parts if not p.children and p.ready <= now]
        urgent = [p for p in able if not p.filler]
        fillers = [p for p in able if p.filler]
        if urgent:
            p = min(urgent, key=lambda p: p.ready)
        elif fillers:
            p = min(fillers, key=lambda p: p.filler)
        else:
            now = min(p.ready for p in parts if not p.children)
            continue
        if p.fresh and len(work.free) < MIN_FREE:
            p.ready = now + 1.0
            continue
        p.fresh = False
        try:
            told = next(p.steps)
        except StopIteration:
            parts.remove(p)
            if p.parent:
                p.parent.children -= 1
                p.parent.ready = max(p.parent.ready, p.ready)
            continue
        if told is Filler:
            p.filler = now + 1e-3
        elif told is Urgent:
            p.filler = False
        elif isinstance(told, list):
            p.children = len(told)
            parts += [Part(steps, p.ready + n * BATCH_STAGGER, p) for n, steps in enumerate(told)]
        else:
            tensor_time, until_next = told
            start = max(now, p.ready)
            now = start + tensor_time
            p.ready = start + until_next


def macaron_program(nc, x_in, w_in, bias_in, const_in, half_in, w1_0, w2_0, w1_1, w2_1, x_out):
    with ExitStack() as ctx:
        def sb(name, shape, dt):
            return ctx.enter_context(nc.sbuf_tensor(name, shape, dt))

        def bank(name, shape=(P, SEQ), dt=F32):
            return ctx.enter_context(nc.psum_tensor(name, list(shape), dt))

        q = Queues(nc, ctx)
        put = q.put

        x_res = [sb(f"x_res{s}", [P, NT, D], F32) for s in range(STREAMS)]
        weights = sb("weights", [P, WCOLS], F32)
        const = sb("const", [P, CCOLS], F32)
        half = sb("half", [P, HALF_KEPT], F16)
        bias = sb("bias", [P, BCOLS], F16)
        blocks = {layer: sb(f"blocks_{layer.name}", [P, layer.E * layer.block], F32) for layer in (L0, L1)}
        expert_block = sb("expert_block", [P, 3 * STREAMS, max(l.block * l.unit for l in (L0, L1))], F32)
        slot_index = [sb(f"slot_index{s}", [P, TOP_K, NT], I32) for s in range(STREAMS)]
        share = [sb(f"share{s}", [P, TOP_K, NT], F32) for s in range(STREAMS)]
        tile_expert = [sb(f"tile_expert{s}", [1, 2, MAX_TILES], I32) for s in range(STREAMS)]
        NWORK, NSMALL = 30, 12
        work_mem = sb("work_mem", [P, NWORK, SEQ], F32)
        small_mem = sb("small_mem", [P, NSMALL, 96], F32)

        work = Slots([work_mem[:, i, :] for i in range(NWORK)], "work")
        block_slots = [Slots([expert_block[:, 3 * s + i, :] for i in range(3)], f"expert_block{s}_") for s in range(STREAMS)]
        small = Slots([small_mem[:, i, :] for i in range(NSMALL)], "small")
        banks = Slots([bank(f"bank{i}")[:, :] for i in range(3)], "bank")
        hidden_banks = Slots([bank(f"hidden_bank{i}")[:, :] for i in range(2)], "hidden_bank")
        out_banks = Slots([bank(f"out_bank{i}")[:, :] for i in range(2)], "out_bank")
        turn_banks = Slots([bank("turn_bank", (P, 2 * SEQ), F16)[:, :]], "turn_bank")

        rows_dram = [nc.dram_tensor(f"rows{s}", [MAX_TILES * P, 2 * D], F16, kind="Internal").ap() for s in range(STREAMS)]
        y_dram = [nc.dram_tensor(f"y{s}", [MAX_TILES * P, D], F32, kind="Internal").ap() for s in range(STREAMS)]
        heads_dram = [nc.dram_tensor(f"heads{i}", [HEADS, D, SEQ // HEADS], F32, kind="Internal").ap() for i in range(BATCHES)]

        def wcol(name):
            return weights[:, WCOL[name][0]:WCOL[name][1]]

        def bcol(name):
            return bias[:, BCOL[name][0]:BCOL[name][1]]

        def ccol(name):
            return const[:, CCOL[name][0]:CCOL[name][1]]

        def hcol(name):
            return half[:, HCOL[name][0]:HCOL[name][1]]

        def block_parts(words, hidden):
            v = words.bitcast(F16)
            return v[:, 0:hidden], v[:, hidden:2 * hidden], v[:, 2 * hidden:2 * hidden + P]

        def block_of(layer, e):
            return block_parts(blocks[layer][:, e * layer.block:(e + 1) * layer.block], layer.H)

        first_select = block_of(L0, 0)[2]

        def tiles(ap, n=BT):
            return ap.rearrange("p (t c) -> p t c", t=n)

        def load(dst, src, name, after=()):
            return put("sync", lambda e: e.dma_start(dst, src), after, name, 16)

        def x_view(ap, s, b):
            return ap[s * SB + b].rearrange("(t p) d -> p t d", p=P)

        x_ready = [[None] * SB for _ in range(STREAMS)]
        for b in range(SB):
            x_ready[0][b] = [load(x_res[0][:, BT * b:BT * b + BT, :], x_view(x_in, 0, b), f"x_loaded0_{b}")]
        const_loaded = load(const[:, :], const_in, "const_loaded")
        weights_loaded = load(weights[:, :], w_in, "weights_loaded")
        load(half[:, :], half_in[:, 0:HALF_KEPT], "half_loaded")
        for layer in (L0, L1):
            dst = blocks[layer][:, :].bitcast(F16).rearrange("p (e c) -> p e c", e=layer.E)[:, :, 2 * layer.H:2 * layer.H + P]
            half_loaded = load(dst, half_in[:, HALF_KEPT:HALF_KEPT + layer.E * P].rearrange("p (e c) -> p e c", c=P), "half_loaded")
        for b in range(SB):
            x_ready[1][b] = [load(x_res[1][:, BT * b:BT * b + BT, :], x_view(x_in, 1, b), f"x_loaded1_{b}")]

        zero = work.take()
        zeroed = put("gpsimd", lambda e: e.memset(zero.ap, 0.0), zero.ready, "zero_done")
        rows_free = []
        for s in range(STREAMS):
            zero_rows = rows_dram[s].rearrange("(n p a) c -> p n (a c)", p=P, a=BT)
            src = zero.ap.bitcast(F16).unsqueeze(1).to_broadcast([P, MAX_TILES // BT, BT * 2 * D])
            rows_free.append([load(zero_rows, src, f"rows_zeroed{s}", [zeroed])])
        work.release(zero, rows_free[0][0], rows_free[1][0])

        def split_biases():
            raw = [work.take() for _ in range(3)]
            high = [work.take() for _ in range(2)]
            ready = [t for r in raw + high for t in r.ready]
            for n, r in enumerate(raw):
                loaded = load(r.ap, bias_in[:, SEQ * n:SEQ * n + SEQ], "bias_loaded", r.ready)
            pieces = []
            for lo, hi, scale in ((0, HIDDEN_BIAS_COLS, X_SCALE * W_SCALE / SEL_VALUE), (HIDDEN_BIAS_COLS, BCOLS, 1 / SEL_VALUE)):
                while lo < hi:
                    end = min(hi, (lo // SEQ + 1) * SEQ)
                    pieces.append((lo, end, scale))
                    lo = end
            clear = put("vector", lambda e: e.memset(bias[:, :], 0.0), (), "bias_step")
            for lo, hi, scale in pieces:
                src = raw[lo // SEQ].ap[:, lo % SEQ:lo % SEQ + hi - lo]
                top = high[lo // 1024].ap.bitcast(F16)[:, lo % 1024:lo % 1024 + hi - lo]
                t = put("vector", lambda e, src=src, top=top, scale=scale: e.tensor_scalar(top, src, scale, None, ALU.mult),
                        [loaded, clear] + ready, "bias_step")
                put("vector", lambda e, top=top, lo=lo, hi=hi: e.tensor_copy(bias[0:LOW_ROW, lo:hi], top[0:LOW_ROW, :]), [t], "bias_step")
                r = slice(LOW_ROW, 2 * LOW_ROW)
                t = put("vector", lambda e, src=src, top=top, lo=lo, hi=hi, scale=scale, r=r:
                        e.scalar_tensor_tensor(bias[r, lo:hi], src[r, :], scale, top[r, :], ALU.mult, ALU.subtract), [t], "bias_step")
            for r in raw + high:
                work.release(r, t)
            return t

        w1_ready = {}

        def split_w1(layer, source, e0, n):
            raw = work.take()
            loaded = load(raw.ap.rearrange("p (e h) -> p e h", e=n), source[e0:e0 + n].rearrange("e d h -> d e h"), raw.name, raw.ready)
            for i in range(n):
                high, low, _ = block_of(layer, e0 + i)
                src = raw.ap[:, i * layer.H:(i + 1) * layer.H]
                t = put("scalar", lambda e: e.activation(high, src, ACT.Copy, scale=W_SCALE), [loaded], "w1_high_done")
                done = put("vector", lambda e: e.scalar_tensor_tensor(low, src, W_SCALE, high, ALU.mult, ALU.subtract), [t, loaded], "w1_low_done")
            work.release(raw, done)
            w1_ready[layer] = [t, done]

        def layer_norm(s, b):
            sm, xn = small.take(), work.take()
            stats, mean_var, rstd = sm.ap[:, 0:24], sm.ap[:, 24:32], sm.ap[:, 32:36]
            x = x_res[s]
            for i in range(BT):
                t = put("vector", lambda e, i=i: e.bn_stats(stats[:, 6 * i:6 * i + 6], x[:, BT * b + i, :]), x_ready[s][b] + sm.ready, f"norm_stats{s}")
            for i in range(BT):
                t2 = put("vector", lambda e, i=i: e.bn_aggr(mean_var[:, 2 * i:2 * i + 2], stats[:, 6 * i:6 * i + 6]), [t], f"norm_stats{s}")
            var, sq = sm.ap[:, 36:40], sm.ap[:, 40:44]

            def step(fn):
                return put("vector", fn, [put_last[0]], f"norm_stats{s}")
            put_last = [t2]
            for fn in [lambda e: e.tensor_scalar(var, mean_var.rearrange("p (t v) -> p t v", v=2)[:, :, 1], EPS, None, ALU.add),
                       lambda e: e.tensor_scalar(rstd.bitcast(I32), var.bitcast(I32), 1, None, ALU.logical_shift_right),
                       lambda e: e.tensor_scalar(rstd.bitcast(I32), rstd.bitcast(I32), -1.0, float(RSQRT_GUESS), ALU.mult, ALU.add),
                       ] + [lambda e: e.tensor_tensor(sq, rstd, rstd, ALU.mult),
                            lambda e: e.scalar_tensor_tensor(sq, sq, -0.5, var, ALU.mult, ALU.mult),
                            lambda e: e.scalar_tensor_tensor(rstd, sq, 1.5, rstd, ALU.add, ALU.mult)] * NEWTON_STEPS:
                put_last[0] = step(fn)
            t3 = put_last[0]
            for i in range(BT):
                t4 = put("vector", lambda e, i=i: e.tensor_scalar(xn.ap[:, D * i:D * i + D], x[:, BT * b + i, :], mean_var[:, 2 * i:2 * i + 1],
                                                                 rstd[:, i:i + 1], ALU.subtract, ALU.mult), [t3] + xn.ready, f"norm_done{s}")
            small.release(sm, t4)
            return xn, t4

        def turn_batch(s, xn, xn_done):
            bk, xt = banks.take(), work.take()

            def go(e):
                for i in range(BT):
                    m = e.transpose(bk.ap[:, P * i:P * i + P], xn.ap[:, D * i:D * i + D], ccol("ident"))
                return m
            turned = put("tensor", go, [xn_done, const_loaded] + bk.ready, f"turned{s}")
            xt_done = put("scalar", lambda e: e.activation(xt.ap, bk.ap, ACT.Copy), [turned] + xt.ready, f"xt_done{s}")
            banks.release(bk, xt_done)
            return xt, xt_done, turned

        state = [dict() for _ in range(STREAMS)]

        def gate_batch(s, b, layer):
            E = layer.E
            gate_w, gate_b = (wcol("gate_w0"), wcol("gate_b0")) if layer is L0 else (wcol("gate_w1"), wcol("gate_b1"))
            st = state[s]
            scores = st["scores"]
            xn, xn_done = layer_norm(s, b)
            yield 0, 6.0
            xt, xt_done, turned = turn_batch(s, xn, xn_done)
            rows = work.take()
            parts = rows.ap.bitcast(F16).rearrange("p (t h d) -> p t h d", t=BT, h=2)
            high = put("scalar", lambda e: e.activation(parts[:, :, 0, :], tiles(xn.ap), ACT.Copy, scale=X_SCALE), [xn_done] + rows.ready, f"rows_high{s}")
            low = put("vector", lambda e: e.scalar_tensor_tensor(parts[:, :, 1, :], tiles(xn.ap), X_SCALE, parts[:, :, 0, :], ALU.mult, ALU.subtract),
                      [high], f"rows_low{s}")
            work.release(xn, turned, high, low)
            st["rows"][b] = (rows, [high, low])
            yield 0.9, 3.0
            bk = banks.take()

            def go(e):
                for i in range(BT):
                    m = e.matmul(bk.ap[:, E * i:E * i + E], xt.ap[:, P * i:P * i + P], gate_w, start=True, stop=True)
                return m
            scored = put("tensor", go, [xt_done, weights_loaded] + bk.ready, f"scored{s}")
            out = scores.ap[:, E * BT * b:E * BT * (b + 1)].rearrange("p (t e) -> p t e", t=BT)
            t = put("vector", lambda e: e.tensor_tensor(out, bk.ap[:, 0:BT * E].rearrange("p (t e) -> p t e", t=BT),
                                                        gate_b.unsqueeze(1).to_broadcast([P, BT, E]), ALU.add), [scored] + scores.ready, f"scores_done{s}")
            banks.release(bk, t)
            st["scores_done"][b] = t
            if layer is L1:
                xt_users = [scored]
                hidden = []
                for c in range(L1.chunks):
                    bk = banks.take()
                    made = put("tensor", lambda e, bk=bk, c=c: e.matmul(bk.ap, wcol("sw1")[:, P * c:P * c + P], xt.ap, start=True, stop=True),
                               [xt_done, weights_loaded] + bk.ready, f"shared_hidden{s}")
                    hs = work.take()
                    done = put("scalar", lambda e, bk=bk, c=c, hs=hs: e.activation(hs.ap, bk.ap, ACT.Gelu, bias=wcol("sb1")[:, c:c + 1]),
                               [made] + hs.ready, f"shared_gelu{s}")
                    banks.release(bk, done)
                    hidden.append((hs, done))
                    xt_users.append(made)
                work.release(xt, *xt_users)
                yield 1.8, 4.0
                bk = banks.take()

                def go(e):
                    for i in range(BT):
                        out = bk.ap[:, D * i:D * i + D]
                        e.matmul(out, first_select, bcol("sb2"), start=True, stop=False)
                        for c in range(L1.chunks):
                            m = e.matmul(out, hidden[c][0].ap[:, P * i:P * i + P], wcol("sw2")[:, D * c:D * c + D], start=False, stop=(c == L1.chunks - 1))
                    return m
                made = put("tensor", go, [h[1] for h in hidden] + [bias_ready[0], half_loaded] + bk.ready, f"shared_out{s}")
                for hs, _ in hidden:
                    work.release(hs, made)
                xb = x_res[s][:, BT * b:BT * b + BT, :]
                t = put("vector", lambda e: e.scalar_tensor_tensor(xb, tiles(bk.ap), 0.5, xb, ALU.mult, ALU.add), [made, xn_done] + x_ready[s][b], f"x_done{s}")
                banks.release(bk, t)
                x_ready[s][b] = [t]
            else:
                work.release(xt, scored)
            yield 2.5, 3.0

        def route(s, layer):
            E = layer.E
            N = E * NT
            st = state[s]
            rev = (ccol("rev0") if layer is L0 else ccol("rev1"))
            sig = f"route{s}"
            scores = st["scores"]
            sm = small.take()
            by_token = "p (t e) -> p t e"
            last = list(st["scores_done"].values()) + sm.ready + [const_loaded]

            def dve(fn, *more):
                t = put("vector", fn, last + list(more), sig)
                last[:] = [t]
                return t

            def over_t(ap):
                return ap.unsqueeze(2).to_broadcast([P, NT, E])

            def over_e(ap):
                return ap.unsqueeze(1).to_broadcast([P, NT, E])

            S = scores.ap[:, 0:N].rearrange(by_token, t=NT)
            if layer is L1:
                top, total = sm.ap[:, 0:NT], sm.ap[:, NT:2 * NT]
                dve(lambda e: e.tensor_reduce(top, S, AX.X, ALU.max))
                dve(lambda e: e.tensor_tensor(S, S, over_t(top), ALU.subtract))
                t = put("scalar", lambda e: e.activation(scores.ap[:, 0:N], scores.ap[:, 0:N], ACT.Exp), last, f"route_exp{s}")
                dve(lambda e: e.tensor_reduce(total, S, AX.X, ALU.add), t)
                dve(lambda e: e.reciprocal(total, total))
                dve(lambda e: e.tensor_tensor(S, S, over_t(total), ALU.mult))
            yield 0, 6.0
            one_hot, tmp = [work.take(), work.take()], work.take()
            value = [sm.ap[:, 2 * NT:3 * NT], sm.ap[:, 3 * NT:4 * NT]]
            pick = sm.ap[:, 4 * NT:5 * NT]
            T = tmp.ap[:, 0:N].rearrange(by_token, t=NT)
            for k in range(TOP_K):
                O = one_hot[k].ap[:, 0:N].rearrange(by_token, t=NT)
                dve(lambda e, k=k: e.tensor_reduce(value[k], S, AX.X, ALU.max))
                dve(lambda e, k=k: e.tensor_tensor(T, S, over_t(value[k]), ALU.is_equal), *tmp.ready)
                dve(lambda e: e.tensor_tensor(T, T, over_e(rev), ALU.mult))
                dve(lambda e: e.tensor_reduce(pick, T, AX.X, ALU.max))
                dve(lambda e, O=O: e.tensor_tensor(O, over_e(rev), over_t(pick), ALU.is_equal), *one_hot[k].ready)
                if k == 0:
                    dve(lambda e, O=O: e.scalar_tensor_tensor(S, O, -3e38, S, ALU.mult, ALU.add))
                yield 0, 4.0
            marks = work.take()
            mark = marks.ap.bitcast(F16)[:, 0:N]
            carry = marks.ap.bitcast(F16)[:, SEQ:SEQ + N]
            mark_v = mark.rearrange("p (e t) -> p t e", e=E)
            dve(lambda e: e.tensor_tensor(mark_v, one_hot[0].ap[:, 0:N].rearrange(by_token, t=NT), one_hot[1].ap[:, 0:N].rearrange(by_token, t=NT), ALU.add), *marks.ready)
            dve(lambda e: e.tensor_tensor_scan(tmp.ap[:, 0:N], ccol("carry")[:, 0:N], mark, 0.0, ALU.mult, ALU.add))
            dve(lambda e: e.tensor_tensor(carry, tmp.ap[:, 0:N], mark, ALU.subtract))
            lastc = marks.ap.bitcast(F16)[:, SEQ - 2 * L0.E:SEQ - 2 * L0.E + E]
            counted = dve(lambda e: e.tensor_copy(lastc, tmp.ap[:, 0:N].rearrange("p (e t) -> p e t", e=E)[:, :, NT - 1]))
            bk = banks.take()

            def go(e):
                e.matmul(bk.ap[:, 0:N], hcol("before"), mark, start=True, stop=False)
                e.matmul(bk.ap[:, 0:N], hcol("ones"), carry, start=False, stop=True)
                return e.matmul(bk.ap[:, N:N + E], hcol("ones"), lastc, start=True, stop=True)
            ranked = put("tensor", go, [counted, half_loaded] + bk.ready, f"ranked{s}")
            yield 0.3, 5.0
            sm2 = small.take()
            need_i = sm2.ap[:, 0:E].bitcast(I32)
            need, end, base = sm2.ap[:, E:2 * E], sm2.ap[:, 2 * E:3 * E], sm2.ap[:, 3 * E:4 * E]
            dve(lambda e: e.tensor_scalar(need_i, bk.ap[:, N:N + E], float(P - 1), None, ALU.add), ranked, *sm2.ready)
            dve(lambda e: e.tensor_scalar(need_i, need_i, P.bit_length() - 1, None, ALU.arith_shift_right))
            dve(lambda e: e.tensor_copy(need, need_i))
            dve(lambda e: e.tensor_tensor_scan(end, hcol("ones")[:, 0:E], need, 0.0, ALU.mult, ALU.add))
            dve(lambda e: e.tensor_tensor(base, end, need, ALU.subtract))
            dve(lambda e: e.tensor_scalar(base, base, float(P), None, ALU.mult))
            R = tmp.ap[:, 0:N].rearrange("p (e t) -> p e t", e=E)
            dve(lambda e: e.tensor_tensor(R, bk.ap[:, 0:N].rearrange("p (e t) -> p e t", e=E), base.unsqueeze(2).to_broadcast([P, E, NT]), ALU.add))
            banks.release(bk, last[0])
            Rt = tmp.ap[:, 0:N].rearrange("p (e t) -> p t e", e=E)
            for k in range(TOP_K):
                O = one_hot[k].ap[:, 0:N].rearrange(by_token, t=NT)
                dve(lambda e, O=O: e.tensor_tensor(O, O, Rt, ALU.mult))
                dve(lambda e, O=O: e.tensor_reduce(pick, O, AX.X, ALU.add))
                indexed = dve(lambda e, k=k: e.tensor_copy(slot_index[s][:, k, :], pick), *st.get("index_free", []))
            yield 0, 5.0
            scattered = []
            for b in range(SB):
                rows, made = st["rows"][b]
                for i in range(BT):
                    for k in range(TOP_K):
                        src = rows.ap.bitcast(F16)[:, 2 * D * i:2 * D * i + 2 * D]
                        at = slot_index[s][:, k, BT * b + i:BT * b + i + 1]
                        t = put("gpsimd", lambda e, src=src, at=at: e.indirect_dma_start(
                            rows_dram[s], bass.IndirectOffsetOnAxis(ap=at, axis=0), src, None), made + [indexed] + rows_free[s], rows.name + "_scattered", 16)
                work.release(rows, t)
                scattered.append(t)
            st["scattered"] = scattered
            ej = sm.ap[:, 0:1]
            dve(lambda e: e.tensor_scalar(need, end, ccol("iota"), None, ALU.is_le))
            dve(lambda e: e.tensor_reduce(ej, need, AX.X, ALU.add))
            named = dve(lambda e: e.tensor_scalar(ej, ej, float(E - 1), None, ALU.min))
            bk = banks.take()
            turned = put("tensor", lambda e: e.matmul(bk.ap[0:1, 0:P], ej, ccol("ident"), start=True, stop=True), [named] + bk.ready, f"ranked{s}")
            dve(lambda e: e.tensor_scalar(tile_expert[s][0:1, 0, 0:layer.tiles], bk.ap[0:1, 0:layer.tiles], float(layer.block), None, ALU.mult), turned, *st.get("expert_free", []))
            dve(lambda e: e.tensor_scalar(tile_expert[s][0:1, 1, 0:layer.tiles], bk.ap[0:1, 0:layer.tiles], 1.0, None, ALU.mult))
            banks.release(bk, last[0])
            st["experts_named"] = last[0]
            if layer is L0:
                gap = sm.ap[:, NT:2 * NT]
                t = dve(lambda e: e.tensor_tensor(gap, value[1], value[0], ALU.subtract))
                t = put("scalar", lambda e: e.activation(gap, gap, ACT.Exp), [t], f"route_exp{s}")
                dve(lambda e: e.tensor_scalar(pick, gap, 1.0, None, ALU.add), t)
                dve(lambda e: e.reciprocal(pick, pick))
                dve(lambda e: e.tensor_scalar(share[s][:, 0, :], pick, 0.5, None, ALU.mult))
                dve(lambda e: e.tensor_tensor(share[s][:, 1, :], share[s][:, 0, :], gap, ALU.mult))
            else:
                for k in range(TOP_K):
                    dve(lambda e, k=k: e.tensor_scalar(share[s][:, k, :], value[k], 0.5, None, ALU.mult))
            st["shared_out"] = last[0]
            for sl in one_hot + [tmp, marks, scores]:
                work.release(sl, last[0])
            small.release(sm, last[0])
            small.release(sm2, last[0])
            yield 0, 36.0

        def experts(s, layer):
            H, C = layer.H, layer.chunks
            st = state[s]
            groups = layer.tiles // BT
            pe_time = layer.unit * layer.chunks * (4 + 4) * PASS_TIME + layer.unit * PASS_TIME
            w2_dram = (w2_0 if layer is L0 else w2_1).rearrange("e (c p) d -> p e c d", p=P)
            b1, b2 = (bcol("b1_0"), bcol("b2_0")) if layer is L0 else (bcol("b1_1"), bcol("b2_1"))
            turned_rows = {}
            rows_read = []
            block_at, w2_at = {}, {}

            def read_tile_experts(g):
                for row, engine, values, top in ((0, VECTOR, block_at, (layer.E - 1) * layer.block), (1, SYNC, w2_at, layer.E - 1)):
                    put(engine, lambda e: None, [st["experts_named"]])
                    _, regs = nc.values_load_multi_w_load_instructions(
                        tile_expert[s][0:1, row, BT * g:BT * g + BT], engines=[ENGINE_TYPE[engine]], min_val=0, max_val=top, skip_runtime_bounds_check_because="the counts keep them in range")
                    for i, r in enumerate(regs):
                        values[BT * g + i] = r

            def bring_weights(unit):
                blk, second = block_slots[s].take(), work.take()
                for j in range(layer.unit):
                    tile = unit * layer.unit + j
                    dst = blk.ap[:, j * layer.block:(j + 1) * layer.block]
                    copied = put("vector", lambda e: e.tensor_copy(dst, blocks[layer][:, bass.ds(block_at[tile], layer.block)]),
                                 w1_ready[layer] + [half_loaded] + blk.ready, f"block_copied{s}")
                    dst2 = second.ap[:, j * H:(j + 1) * H].rearrange("p (o c d) -> p o c d", o=1, c=C)
                    landed = load(dst2, w2_dram[:, bass.ds(w2_at[tile], 1)], second.name, second.ready)
                return blk, copied, second, landed

            def fetch(g):
                rows = work.take()
                src = rows_dram[s][g * BT * P:(g + 1) * BT * P].rearrange("(t p) c -> p t c", p=P)
                t = load(rows.ap.bitcast(F16).rearrange("p (t c) -> p t c", t=BT), src, rows.name, st["scattered"] + rows.ready)
                rows_read.append(t)
                return rows, t

            def turn(g, rows, loaded):
                bk, xt = turn_banks.take(), work.take()
                R = rows.ap.bitcast(F16).rearrange("p (n d) -> p n d", d=D)

                def go(e):
                    for n in range(2 * BT):
                        m = e.transpose(bk.ap[:, P * n:P * n + P], R[:, n, :], hcol("ident"))
                    return m
                turned = put("tensor", go, [loaded, half_loaded] + bk.ready, f"rows_turned{s}")
                work.release(rows, turned)
                done = put("scalar", lambda e: e.activation(xt.ap.bitcast(F16), bk.ap, ACT.Copy), [turned] + xt.ready, f"rows_xt{s}")
                turn_banks.release(bk, done)
                turned_rows[g] = (xt, done)

            yield Filler
            fetched = [fetch(0), fetch(1)]
            read_tile_experts(0)
            brought = [bring_weights(0), bring_weights(1)]
            units = layer.tiles // layer.unit
            turn(0, *fetched[0])
            pending = None
            out_bank = None
            users = []
            y_stored = None
            for unit in range(units):
                first = unit * layer.unit
                g = first // BT
                if first % BT == 0:
                    if g + 2 < groups:
                        fetched.append(fetch(g + 2))
                xt, xt_done = turned_rows[g]
                hb, hid = hidden_banks.take(), work.take()

                blk, copied, second, landed = brought[unit]

                def layer1(e):
                    X = xt.ap.bitcast(F16).rearrange("p (t h n) -> p t h n", t=BT, h=2)
                    for j in range(layer.unit):
                        xh, xl = X[:, (first + j) % BT, 0, :], X[:, (first + j) % BT, 1, :]
                        high, low, select = block_parts(blk.ap[:, j * layer.block:(j + 1) * layer.block], H)
                        for c in range(C):
                            out = hb.ap[:, j * H + c * P:j * H + c * P + P]
                            e.matmul(out, b1[:, c * P:c * P + P], select, start=True, stop=False)
                            e.matmul(out, high[:, c * P:c * P + P], xh, start=False, stop=False)
                            e.matmul(out, high[:, c * P:c * P + P], xl, start=False, stop=False)
                            m = e.matmul(out, low[:, c * P:c * P + P], xh, start=False, stop=True)
                    return m
                made = put("tensor", layer1, [xt_done, copied, bias_ready[0]] + hb.ready, f"hidden_made{s}")
                if (first + layer.unit) % BT == 0:
                    work.release(xt, made)
                gelu = put("scalar", lambda e, hb=hb, hid=hid: e.activation(hid.ap, hb.ap, ACT.Gelu, scale=1 / (X_SCALE * W_SCALE)),
                           [made] + hid.ready, f"hidden_gelu{s}")
                hidden_banks.release(hb, gelu)
                if first % BT == BT // 2 and g + 1 < groups:
                    turn(g + 1, *fetched[g + 1])
                ripe = ([pending] if pending else []) + ([(first, hid, gelu, brought[unit])] if unit == units - 1 else [])
                for first2, hid2, gelu2, (blk2, copied2, second2, landed2) in ripe:
                    if first2 % BT == 0:
                        out_bank = out_banks.take()

                    def layer2(e):
                        for j in range(layer.unit):
                            out = out_bank.ap[:, D * ((first2 + j) % BT):D * ((first2 + j) % BT) + D]
                            select = block_parts(blk2.ap[:, j * layer.block:(j + 1) * layer.block], H)[2]
                            e.matmul(out, select, b2, start=True, stop=False)
                            for c in range(C):
                                at = slice(j * H + c * P, j * H + c * P + P)
                                m = e.matmul(out, hid2.ap[:, at], second2.ap[:, at], start=False, stop=(c == C - 1))
                        return m
                    done = put("tensor", layer2, [gelu2, landed2, copied2] + out_bank.ready, f"expert_out{s}")
                    block_slots[s].release(blk2, done)
                    work.release(second2, done)
                    work.release(hid2, done)
                    if (first2 + layer.unit) % BT == 0:
                        g2 = first2 // BT
                        y = work.take()
                        copied = put("vector", lambda e, ob=out_bank, y=y: e.tensor_copy(y.ap, ob.ap), [done] + y.ready, f"y_copied{s}")
                        out_banks.release(out_bank, copied)
                        dst = y_dram[s][g2 * BT * P:(g2 + 1) * BT * P].rearrange("(t p) d -> p t d", p=P)
                        y_stored = put("sync", lambda e, dst=dst, y=y: e.dma_start(dst, tiles(y.ap)), [copied] + st.get("y_free", []), y.name, 16)
                        work.release(y, y_stored)
                        users.append(y_stored)
                pending = (first, hid, gelu, brought[unit])
                if unit + 2 < units:
                    if (unit + 2) * layer.unit % BT == 0:
                        read_tile_experts((unit + 2) * layer.unit // BT)
                    brought.append(bring_weights(unit + 2))
                yield pe_time, pe_time
            rows_free[s] = rows_read
            st["expert_free"] = [copied, landed]
            st["y_stored"] = users
            st["y_free"], st["index_free"] = [], []

        def combine_batch(s, b):
            st = state[s]
            x = x_res[s]
            gathered = []
            for pair in range(BT // 2):
                got = work.take()
                for i in range(2):
                    for k in range(TOP_K):
                        t, col = BT * b + 2 * pair + i, D * (2 * i + k)
                        at = slot_index[s][:, k, t:t + 1]
                        landed = put("gpsimd", lambda e, got=got, col=col, at=at: e.indirect_dma_start(
                            got.ap[:, col:col + D], None, y_dram[s], bass.IndirectOffsetOnAxis(ap=at, axis=0)),
                            st["y_stored"] + got.ready, got.name + "_gathered", 16)
                        gathered.append((t, k, got, col))
                got.landed = landed
                st["y_free"].append(landed)
                st["index_free"].append(landed)
            yield 0, GATHER_TIME * TOP_K * BT + 3.0
            for t, k, got, col in gathered:
                done = put("vector", lambda e, t=t, k=k, col=col, got=got: e.scalar_tensor_tensor(
                    x[:, t, :], got.ap[:, col:col + D], share[s][:, k, t:t + 1], x[:, t, :], ALU.mult, ALU.add),
                    [got.landed, st["shared_out"]] + x_ready[s][b], f"x_done{s}")
                x_ready[s][b] = [done]
                if col == SEQ - D:
                    work.release(got, done)
            yield 0, 2.0

        def linear_attention(s, b):
            xn, xn_done = layer_norm(s, b)
            yield 0, 6.0
            xt, xt_done, turned = turn_batch(s, xn, xn_done)
            work.release(xn, turned)
            yield 0.9, 3.0
            first = {}
            for name, mat, bi in (("q", "q1", "q_b1"), ("k", "k1", "k_b1"), ("v", "v", "v_b"), ("g", "g", "g_b")):
                bk, out = banks.take(), work.take()
                made = put("tensor", lambda e, bk=bk, mat=mat: e.matmul(bk.ap, wcol(mat), xt.ap, start=True, stop=True),
                           [xt_done, weights_loaded] + bk.ready, f"attn_made{s}")
                done = put("scalar", lambda e, bk=bk, out=out, bi=bi: e.activation(out.ap, bk.ap, ACT.Gelu, bias=wcol(bi)), [made] + out.ready, f"attn_gelu{s}")
                banks.release(bk, done)
                first[name] = (out, done)
                if name == "k":
                    yield 1.7, 2.0
            work.release(xt, made)
            yield 1.7, 3.0
            second = {}
            zs = []
            for name, mat, bi in (("q", "q2", "q_b2"), ("k", "k2", "k_b2")):
                hid, hid_done = first[name]
                bk, z, mag = banks.take(), work.take(), work.take()

                def go(e, bk=bk, hid=hid, mat=mat, bi=bi):
                    for i in range(BT):
                        out = bk.ap[:, D * i:D * i + D]
                        e.matmul(out, first_select, bcol(bi), start=True, stop=False)
                        m = e.matmul(out, hid.ap[:, P * i:P * i + P], wcol(mat), start=False, stop=True)
                    return m
                made = put("tensor", go, [hid_done, bias_ready[0], half_loaded] + bk.ready, f"attn_made{s}")
                work.release(hid, made)
                pos = put("vector", lambda e, bk=bk, z=z: e.tensor_scalar(z.ap, bk.ap, 0.0, None, ALU.max), [made] + z.ready, f"attn_dve{s}")
                size = put("vector", lambda e, bk=bk, z=z, mag=mag: e.scalar_tensor_tensor(mag.ap, z.ap, -2.0, bk.ap, ALU.mult, ALU.add),
                           [pos] + mag.ready, f"attn_dve{s}")
                banks.release(bk, size)
                zs.append((name, z, mag, size))
            yield 1.0, 3.0
            exps = []
            for name, z, mag, size in zs:
                exps.append(put("scalar", lambda e, mag=mag: e.activation(mag.ap, mag.ap, ACT.Exp), [size], f"attn_exp{s}"))
            for (name, z, mag, size), ex in zip(zs, exps):
                ln = put("scalar", lambda e, mag=mag: e.activation(mag.ap, mag.ap, ACT.Ln, bias=ccol("one")), [ex, const_loaded], f"attn_exp{s}")
                done = put("vector", lambda e, z=z, mag=mag: e.tensor_tensor(z.ap, z.ap, mag.ap, ALU.add), [ln], f"attn_dve{s}")
                work.release(mag, done)
                second[name] = (z, done)
            yield 1.0, 4.0
            (qs, q_done), (ks, k_done) = second["q"], second["k"]
            bk, sm, at_ = banks.take(), small.take(), work.take()

            def go(e):
                for i in range(BT):
                    m = e.matmul(bk.ap[:, 0:D], ks.ap[:, D * i:D * i + D], qs.ap[:, D * i:D * i + D], start=(i == 0), stop=(i == BT - 1))
                return m
            made = put("tensor", go, [q_done, k_done] + bk.ready, f"attn_made{s}")
            work.release(qs, made)
            work.release(ks, made)
            heads = at_.ap[:, 0:D]
            masked = put("vector", lambda e: e.tensor_tensor(heads, bk.ap[:, 0:D], ccol("heads"), ALU.mult), [made, const_loaded] + at_.ready, f"attn_dve{s}")
            banks.release(bk, masked)
            yield 0.9, 2.0
            (vt, v_done), (gt, g_done) = first["v"], first["g"]
            bk, bk2 = banks.take(), banks.take()
            summed = put("tensor", lambda e: e.matmul(bk2.ap[:, 0:1], heads, ccol("one"), start=True, stop=True), [masked] + bk2.ready, f"attn_made{s}")
            made = put("tensor", lambda e: e.matmul(bk.ap, heads, vt.ap, start=True, stop=True), [v_done] + bk.ready, f"attn_made{s}")
            z1, z2 = sm.ap[:, 0:1], sm.ap[:, 1:2]
            t = put("vector", lambda e: e.tensor_scalar(z1, bk2.ap[:, 0:1], float(D), None, ALU.add), [summed] + sm.ready, f"attn_dve{s}")
            banks.release(bk2, t)
            zinv = put("vector", lambda e: e.reciprocal(z2, z1), [t], f"attn_dve{s}")
            t = put("vector", lambda e: e.tensor_tensor(vt.ap, bk.ap, vt.ap, ALU.add), [made], f"attn_dve{s}")
            banks.release(bk, t)
            work.release(at_, made)
            o = work.take()
            o_view = o.ap.rearrange("p (c a) -> p a c", a=SEQ // HEADS)
            gated = put("vector", lambda e: e.scalar_tensor_tensor(o_view, vt.ap.rearrange("p (a c) -> p a c", c=HEADS), z2,
                                                                   gt.ap.rearrange("p (a c) -> p a c", c=HEADS), ALU.mult, ALU.mult),
                        [t, zinv, g_done] + o.ready, f"attn_dve{s}")
            small.release(sm, gated)
            work.release(vt, gated)
            work.release(gt, gated)
            hd = heads_dram[s * SB + b]
            stored = put("sync", lambda e: e.dma_start(hd.rearrange("c p a -> p c a"), o.ap.rearrange("p (c a) -> p c a", c=HEADS)), [gated], o.name, 16)
            work.release(o, stored)
            m = work.take()
            landed = load(m.ap, hd.rearrange("c (n h) a -> (c n) (h a)", h=HEADS), m.name, [stored] + m.ready)
            yield 1.1, 12.0
            bk = banks.take()

            def go2(e):
                for i in range(BT):
                    out = bk.ap[:, D * i:D * i + D]
                    e.matmul(out, first_select, bcol("p_b"), start=True, stop=False)
                    mm = e.matmul(out, m.ap[:, P * i:P * i + P], wcol("p"), start=False, stop=True)
                return mm
            made = put("tensor", go2, [landed] + bk.ready, f"attn_made{s}")
            work.release(m, made)
            xb = x_res[s][:, BT * b:BT * b + BT, :]
            t = put("vector", lambda e: e.tensor_tensor(xb, tiles(bk.ap), xb, ALU.add), [made, xn_done] + x_ready[s][b], f"x_done{s}")
            banks.release(bk, t)
            x_ready[s][b] = [t]
            yield 1.0, 2.0

        def causal_attention(s, b):
            xn, xn_done = layer_norm(s, b)
            yield 0, 6.0
            xt, xt_done, turned = turn_batch(s, xn, xn_done)
            work.release(xn, turned)
            yield 0.9, 3.0
            roped = []
            for mat in ("wq", "wk"):
                parts = []
                for m_name, table in ((mat, "cos"), (mat + "_swap", "sin")):
                    bk, out = banks.take(), work.take()
                    made = put("tensor", lambda e, bk=bk, m_name=m_name: e.matmul(bk.ap, wcol(m_name), xt.ap, start=True, stop=True),
                               [xt_done, weights_loaded] + bk.ready, f"attn_made{s}")
                    done = put("vector", lambda e, bk=bk, out=out, table=table: e.tensor_tensor(out.ap, bk.ap, ccol(table), ALU.mult),
                               [made, const_loaded] + out.ready, f"attn_dve{s}")
                    banks.release(bk, done)
                    parts.append((out, done))
                (a, a_done), (c, c_done) = parts
                done = put("gpsimd", lambda e, a=a, c=c: e.tensor_tensor(a.ap, a.ap, c.ap, ALU.add), [a_done, c_done], f"roped{s}")
                work.release(c, done)
                roped.append((a, done))
                yield 1.7, 2.5
            bk, v = banks.take(), work.take()

            def go(e):
                for i in range(BT):
                    m = e.matmul(bk.ap[:, D * i:D * i + D], xt.ap[:, P * i:P * i + P], wcol("wv"), start=True, stop=True)
                return m
            made = put("tensor", go, [xt_done] + bk.ready, f"attn_made{s}")
            work.release(xt, made)
            v_done = put("scalar", lambda e: e.activation(v.ap, bk.ap, ACT.Copy), [made] + v.ready, f"attn_copy{s}")
            banks.release(bk, v_done)
            yield 0.9, 1.5
            (qt, q_done), (kt, k_done) = roped
            sm = small.take()
            for i in range(BT):
                n = P * (i + 1)
                top, neg, total, inv = (sm.ap[:, 4 * i + j:4 * i + j + 1] for j in range(4))
                bk, pr = banks.take(), work.take()
                made = put("tensor", lambda e, bk=bk, i=i, n=n: e.matmul(bk.ap[:, 0:n], qt.ap[:, P * i:P * i + P], kt.ap[:, 0:n], start=True, stop=True),
                           [q_done, k_done] + bk.ready, f"attn_made{s}")
                diag = bk.ap[:, P * i:n]
                t = put("vector", lambda e, diag=diag: e.tensor_tensor(diag, diag, ccol("causal"), ALU.add), [made], f"attn_dve{s}")
                t = put("vector", lambda e, bk=bk, n=n, top=top: e.tensor_reduce(top, bk.ap[:, 0:n], AX.X, ALU.max), [t] + sm.ready, f"attn_dve{s}")
                t = put("vector", lambda e, top=top, neg=neg: e.tensor_scalar(neg, top, -ATTN_SCALE, None, ALU.mult), [t], f"attn_dve{s}")
                ex = put("scalar", lambda e, bk=bk, pr=pr, n=n, neg=neg, total=total: e.activation(
                    pr.ap[:, 0:n], bk.ap[:, 0:n], ACT.Exp, bias=neg, scale=ATTN_SCALE, accum_out=total), [t] + pr.ready, f"attn_exp{s}")
                banks.release(bk, ex)
                yield 0.6, 4.0
                bk, prt = banks.take(), work.take()

                def go(e, bk=bk, pr=pr, i=i):
                    for j in range(i + 1):
                        m = e.transpose(bk.ap[:, P * j:P * j + P], pr.ap[:, P * j:P * j + P], ccol("ident"))
                    return m
                turned = put("tensor", go, [ex] + bk.ready, f"attn_made{s}")
                work.release(pr, turned)
                copied = put("scalar", lambda e, bk=bk, prt=prt, n=n: e.activation(prt.ap[:, 0:n], bk.ap[:, 0:n], ACT.Copy), [turned] + prt.ready, f"attn_copy{s}")
                banks.release(bk, copied)
                r = put("vector", lambda e, total=total, inv=inv: e.reciprocal(inv, total), [ex], f"attn_dve{s}")
                yield 0.5, 3.0
                bk = banks.take()

                def go(e, bk=bk, prt=prt, i=i):
                    for j in range(i + 1):
                        m = e.matmul(bk.ap[:, 0:D], prt.ap[:, P * j:P * j + P], v.ap[:, D * j:D * j + D], start=(j == 0), stop=(j == i))
                    return m
                made = put("tensor", go, [copied, v_done] + bk.ready, f"attn_made{s}")
                work.release(prt, made)
                xi = x_res[s][:, BT * b + i, :]
                t = put("vector", lambda e, bk=bk, xi=xi, inv=inv: e.scalar_tensor_tensor(xi, bk.ap[:, 0:D], inv, xi, ALU.mult, ALU.add),
                        [made, r, xn_done] + x_ready[s][b], f"x_done{s}")
                banks.release(bk, t)
                yield 0.5, 0.5
            x_ready[s][b] = [t]
            small.release(sm, t)
            for sl in (qt, kt, v):
                work.release(sl, made)

        bias_ready = [None]

        def prepare_weights():
            yield 0, 12.0
            bias_ready[0] = split_biases()
            yield 0, 8.0
            for e in range(L0.E):
                split_w1(L0, w1_0, e, 1)
                yield 0, 1.6
            yield 0, 100.0
            for e in range(0, L1.E, L1.unit):
                split_w1(L1, w1_1, e, L1.unit)
                yield 0, 4.0

        def batch(s, b, *parts):
            for part, *args in parts:
                yield from part(s, b, *args)

        def new_scores(s):
            state[s]["scores"], state[s]["rows"], state[s]["scores_done"] = work.take(), {}, {}

        def store_batch(s, b):
            put("sync", lambda e: e.dma_start(x_view(x_out, s, b), x_res[s][:, BT * b:BT * b + BT, :]), x_ready[s][b], "x_stored", 16)
            yield 0, 0

        def stream(s):
            yield 0, STREAM_DELAY * s
            for layer, *before in ((L0,), (L0, (combine_batch,), (linear_attention,)), (L1, (combine_batch,)),
                                   (L1, (combine_batch,), (causal_attention,))):
                new_scores(s)
                yield [batch(s, b, *before, (gate_batch, layer)) for b in range(SB)]
                yield from route(s, layer)
                yield from experts(s, layer)
                yield Urgent
                yield 0, 3.0
            yield [batch(s, b, (combine_batch,), (store_batch,)) for b in range(SB)]

        interleave([stream(0), stream(1), prepare_weights()], work)

        written = [Token(name, q.count[name]) for name in q.sems if name.startswith("work") or name in ("x_stored", "rows_zeroed0", "rows_zeroed1")]
        put("sync", lambda e: None, written)


def constants():
    f = np.float32
    c = np.zeros((P, CCOLS), f)

    def put(name, value):
        c[:, CCOL[name][0]:CCOL[name][1]] = value
    r = np.arange(P)
    put("ident", np.eye(P, dtype=f))
    put("heads", (r[:, None] % HEADS == r[None, :] % HEADS) * f(HEAD_SCALE))
    put("causal", np.where(r[None, :] > r[:, None], f(-1e30), f(0)))
    inv_freq = f(1) / f(10000.0) ** (np.arange(0, D, 2, dtype=f) / f(D))
    freqs = np.arange(SEQ, dtype=f)[:, None] * inv_freq
    put("cos", np.repeat(np.cos(freqs), 2, axis=-1).T)
    put("sin", np.repeat(np.sin(freqs), 2, axis=-1).T * np.where(r % 2 == 0, f(-1), f(1))[:, None])
    put("carry", np.tile((np.arange(NT) > 0).astype(f), L0.E)[None, :])
    put("rev0", (L0.E - np.arange(L0.E)).astype(f)[None, :])
    put("rev1", (L1.E - np.arange(L1.E)).astype(f)[None, :])
    put("iota", r[:, None])
    put("one", 1)
    h = np.zeros((P, HCOLS), np.float16)
    h[:, HCOL["ident"][0]:HCOL["ident"][1]] = np.eye(P)
    h[:, HCOL["before"][0]:HCOL["before"][1]] = r[:, None] < r[None, :]
    h[:, HCOL["ones"][0]:HCOL["ones"][1]] = 1
    sel = np.zeros((P, L0.E, P), np.float16)
    for e in range(L0.E):
        sel[e, e, :] = sel[LOW_ROW + e, e, :] = SEL_VALUE
    h[:, HCOL["select"][0]:HCOL["select"][1]] = sel.reshape(P, -1)
    return c, h


def kernel(**inputs):
    import concourse.bacc as bacc
    from concourse.bass_utils import run_bass_kernel_spmd

    a = {k: np.asarray(v) for k, v in inputs.items()}
    swap = np.arange(D) ^ 1
    turn = np.arange(D).reshape(HEADS, HEAD_DIM).T.ravel()
    mats = {"q1": a["L0_attn_q_w1"], "k1": a["L0_attn_k_w1"], "v": a["L0_attn_v_w"][turn], "g": a["L0_attn_g_w"][turn],
            "q2": a["L0_attn_q_w2"][turn], "k2": a["L0_attn_k_w2"][turn], "p": a["L0_attn_p_w"],
            "wq": a["L1_attn_wq"], "wq_swap": a["L1_attn_wq"][swap], "wk": a["L1_attn_wk"], "wk_swap": a["L1_attn_wk"][swap],
            "wv": a["L1_attn_wv"]}
    w = np.zeros((P, WCOLS), np.float32)
    for name, m in mats.items():
        w[:, WCOL[name][0]:WCOL[name][1]] = m.T
    for name, m in (("gate_w0", a["L0_ffn_gate_w"]), ("gate_w1", a["L1_ffn_router_w"]),
                    ("gate_b0", a["L0_ffn_gate_b"][None, :]), ("gate_b1", a["L1_ffn_router_b"][None, :]), ("sw1", a["L1_ffn_sw1"]),
                    ("sw2", a["L1_ffn_sw2"].reshape(L1.chunks, P, D).transpose(1, 0, 2).reshape(P, -1)),
                    ("q_b1", a["L0_attn_q_b1"][:, None]), ("k_b1", a["L0_attn_k_b1"][:, None]), ("v_b", a["L0_attn_v_b"][turn][:, None]),
                    ("g_b", a["L0_attn_g_b"][turn][:, None]), ("sb1", a["L1_ffn_sb1"].reshape(L1.chunks, P).T)):
        w[:, WCOL[name][0]:WCOL[name][1]] = m
    rows = np.zeros((P, BCOLS), np.float32)
    for name, m in (("b1_0", a["L0_ffn_b1"]), ("b1_1", a["L1_ffn_rb1"]), ("b2_0", a["L0_ffn_b2"]), ("b2_1", a["L1_ffn_rb2"]),
                    ("q_b2", a["L0_attn_q_b2"][turn][None, :]), ("k_b2", a["L0_attn_k_b2"][turn][None, :]), ("p_b", a["L0_attn_p_b"][None, :]),
                    ("sb2", a["L1_ffn_sb2"][None, :])):
        for at in (0, LOW_ROW):
            rows[at:at + m.shape[0], BCOL[name][0]:BCOL[name][1]] = m
    c, h = constants()
    arrays = {"x": a["L0_attn_x"], "w": w, "bias_rows": rows, "const": c, "half": h, "w1_0": a["L0_ffn_w1"], "w2_0": a["L0_ffn_w2"],
              "w1_1": a["L1_ffn_rw1"], "w2_1": a["L1_ffn_rw2"]}
    arrays = {f"in_{k}_dram": np.ascontiguousarray(v) for k, v in arrays.items()}
    nc = bacc.Bacc("TRN2", target_bir_lowering=False, num_devices=1)
    args = [nc.dram_tensor(k, v.shape, mybir.dt.from_np(v.dtype), kind="ExternalInput").ap() for k, v in arrays.items()]
    args.append(nc.dram_tensor("out_0_dram", (BATCHES, SEQ, D), F32, kind="ExternalOutput").ap())
    macaron_program(nc, *args)
    r = run_bass_kernel_spmd(nc, [arrays], core_ids=[0])
    return r.results[0]["out_0_dram"]
```

```python
from contextlib import ExitStack

import concourse.bass as bass
import numpy as np
from concourse import mybir

F32 = mybir.dt.float32
F16 = mybir.dt.float16
I32 = mybir.dt.int32
ALU = mybir.AluOpType
ACT = mybir.ActivationFunctionType
AX = mybir.AxisListType
VECTOR, SYNC = "vector", "sync"
ENGINE_TYPE = {VECTOR: mybir.EngineType.DVE, SYNC: mybir.EngineType.SP}

P = 128
D = 128
BATCHES, SEQ = 8, 512
STREAMS = 2
SB = BATCHES // STREAMS
BT = SEQ // P
NT = SB * BT
TOP_K = 2
EPS = 1e-5
RSQRT_GUESS = 0x5F3759DF
NEWTON_STEPS = 3

HEADS = 16
HEAD_DIM = D // HEADS
HEAD_SCALE = HEAD_DIM ** -0.5
ATTN_SCALE = D ** -0.5

X_SCALE = 32.0
W_SCALE = 32.0
SEL_VALUE = 4.0
LOW_ROW = 32

WEIGHTS_AHEAD = 3
HIDDEN_AHEAD = 2
LOAD_GROUPS = 2

PASS_TIME = 0.0535
INDIRECT_TIME = 1.04
BATCH_STAGGER = 8.4
STREAM_DELAY = 40.0
LAST_COMBINE_DELAY = 50.0
MIN_FREE = 14


class Layer:

    def __init__(self, name, experts, hidden):
        self.name, self.E, self.H = name, experts, hidden
        self.chunks = hidden // P
        pairs = NT * P * TOP_K
        bound = (pairs - experts) // P + experts
        self.tiles = -(-bound // BT) * BT
        self.unit = SEQ // hidden
        self.block = hidden + P // 2 + self.chunks


L0 = Layer("l0", 24, 512)
L1 = Layer("l1", 8, 256)
MAX_TILES = max(L0.tiles, L1.tiles)

MATS = ["q1", "k1", "v", "g", "q2", "k2", "p", "wq", "wq_swap", "wk", "wk_swap", "wv"]


def columns(widths):
    at, out = 0, {}
    for name, n in widths:
        out[name] = (at, at + n)
        at += n
    return out, at


WCOL, WCOLS = columns([(m, D) for m in MATS] + [
    ("gate_w0", L0.E), ("gate_w1", L1.E), ("gate_b0", L0.E), ("gate_b1", L1.E),
    ("sw1", L1.H), ("sw2", L1.chunks * D), ("q_b1", 1), ("k_b1", 1), ("v_b", 1), ("g_b", 1), ("sb1", L1.chunks),
    ("b1_0", L0.E * L0.chunks), ("b1_1", L1.E * L1.chunks)])
BCOL, BCOLS = columns([("b2_0", D), ("b2_1", D), ("q_b2", D), ("k_b2", D), ("p_b", D), ("sb2", D)])
CCOL, CCOLS = columns([("ident", P), ("heads", D), ("causal", P), ("cos", SEQ), ("sin", SEQ),
                       ("carry", L0.E * NT), ("rev0", L0.E), ("rev1", L1.E), ("iota", 1), ("one", 1)])
HCOL, HCOLS = columns([("ident", P), ("before", P), ("ones", P), ("select", L0.E * P)])
HALF_KEPT = HCOL["select"][0]


class Token:

    def __init__(self, sem, value):
        self.sem, self.value = sem, value


class Queues:

    def __init__(self, nc, ctx):
        self.nc, self.ctx = nc, ctx
        self.sems, self.count = {}, {}
        self.engines = {"tensor": nc.tensor, "vector": nc.vector, "scalar": nc.scalar, "gpsimd": nc.gpsimd, "sync": nc.sync}
        self.waited = {e: {} for e in self.engines}

    def put(self, engine, work, after, signal=None, by=1):
        waits = []
        seen = self.waited[engine]
        best = {}
        for t in after:
            best[t.sem] = max(best.get(t.sem, 0), t.value)
        for name, value in best.items():
            if seen.get(name, 0) < value:
                seen[name] = value
                waits.append((name, value))
        if signal is not None:
            if signal not in self.sems:
                self.sems[signal] = self.ctx.enter_context(self.nc.semaphore(signal))
                self.count[signal] = 0
            self.count[signal] += by
        eng = self.engines[engine]
        for name, value in waits:
            eng.wait_ge(self.sems[name], value)
        last = work(eng)
        if signal is not None:
            last.then_inc(self.sems[signal], by)
        return Token(signal, self.count[signal]) if signal is not None else None


class Slot:
    def __init__(self, ap, name):
        self.ap, self.name, self.ready = ap, name, []


class Slots:

    def __init__(self, aps, name):
        self.free = [Slot(ap, f"{name}{i}") for i, ap in enumerate(aps)]

    def take(self):
        return self.free.pop(0)

    def release(self, slot, *tokens):
        slot.ready = list(tokens)
        self.free.append(slot)


FILLER = "filler"
URGENT = "urgent"
GPSIMD_IDLE = "gpsimd idle"


class Part:
    def __init__(self, steps, ready, parent=None):
        self.steps, self.ready, self.parent = steps, ready, parent
        self.filler_since, self.children, self.fresh, self.wants_gpsimd = None, 0, parent is not None, False


def interleave(streams, work):
    now, gpsimd_free = 0.0, 0.0
    parts = [Part(steps, 0.0) for steps in streams]

    def due(p):
        return max(p.ready, gpsimd_free - 1.0) if p.wants_gpsimd else p.ready

    while parts:
        able = [p for p in parts if not p.children and due(p) <= now]
        urgent = [p for p in able if p.filler_since is None]
        if urgent:
            p = min(urgent, key=lambda p: p.ready)
        elif able:
            p = min(able, key=lambda p: p.filler_since)
        else:
            now = min(due(p) for p in parts if not p.children)
            continue
        if p.fresh and len(work.free) < MIN_FREE:
            p.ready = now + 1.0
            continue
        p.fresh = p.wants_gpsimd = False
        try:
            told = next(p.steps)
        except StopIteration:
            parts.remove(p)
            if p.parent:
                p.parent.children -= 1
                p.parent.ready = max(p.parent.ready, p.ready)
            continue
        if told is FILLER:
            p.filler_since = now
        elif told is URGENT:
            p.filler_since = None
        elif told is GPSIMD_IDLE:
            p.wants_gpsimd = True
        elif isinstance(told, list):
            p.children = len(told)
            parts += [Part(steps, p.ready + n * BATCH_STAGGER, p) for n, steps in enumerate(told)]
        else:
            tensor_time, until_next, *gpsimd_time = told
            start = max(now, p.ready)
            now = start + tensor_time
            if gpsimd_time:
                start = gpsimd_free = max(gpsimd_free, start) + gpsimd_time[0]
            p.ready = start + until_next


def macaron_program(nc, x_in, w_in, bias_in, const_in, half_in, w1_0, w2_0, w1_1, w2_1, x_out):
    with ExitStack() as ctx:
        def sb(name, shape, dt):
            return ctx.enter_context(nc.sbuf_tensor(name, shape, dt))

        def bank(name, shape=(P, SEQ), dt=F32):
            return ctx.enter_context(nc.psum_tensor(name, list(shape), dt))

        q = Queues(nc, ctx)
        put = q.put

        x_res = [sb(f"x_res{s}", [P, NT, D], F32) for s in range(STREAMS)]
        weights = sb("weights", [P, WCOLS], F32)
        const = sb("const", [P, CCOLS], F32)
        half = sb("half", [P, HALF_KEPT], F16)
        bias = sb("bias", [P, BCOLS], F16)
        blocks = {layer: sb(f"blocks_{layer.name}", [P, layer.E * layer.block], F32) for layer in (L0, L1)}
        NWORK, NSMALL, NBLOCK = 36, 12, 7
        expert_block = sb("expert_block", [P, NBLOCK, max(l.block * l.unit for l in (L0, L1))], F32)
        slot_index = [sb(f"slot_index{s}", [P, TOP_K, NT], I32) for s in range(STREAMS)]
        share = [sb(f"share{s}", [P, TOP_K, NT], F32) for s in range(STREAMS)]
        tile_expert = [sb(f"tile_expert{s}", [1, 2, MAX_TILES], I32) for s in range(STREAMS)]
        work_mem = sb("work_mem", [P, NWORK, SEQ], F32)
        small_mem = sb("small_mem", [P, NSMALL, 96], F32)

        work = Slots([work_mem[:, i, :] for i in range(NWORK)], "work")
        block_slots = Slots([expert_block[:, i, :] for i in range(NBLOCK)], "expert_block")
        small = Slots([small_mem[:, i, :] for i in range(NSMALL)], "small")
        banks = Slots([bank(f"bank{i}")[:, :] for i in range(3)], "bank")
        hidden_banks = Slots([bank(f"hidden_bank{i}")[:, :] for i in range(2)], "hidden_bank")
        out_banks = Slots([bank(f"out_bank{i}")[:, :] for i in range(2)], "out_bank")
        turn_banks = Slots([bank("turn_bank", (P, 2 * SEQ), F16)[:, :]], "turn_bank")

        rows_dram = [nc.dram_tensor(f"rows{s}", [MAX_TILES * P, 2 * D], F16, kind="Internal").ap() for s in range(STREAMS)]
        y_dram = [nc.dram_tensor(f"y{s}", [MAX_TILES * P, D], F32, kind="Internal").ap() for s in range(STREAMS)]
        heads_dram = [nc.dram_tensor(f"heads{i}", [HEADS, D, SEQ // HEADS], F32, kind="Internal").ap() for i in range(BATCHES)]

        def wcol(name):
            return weights[:, WCOL[name][0]:WCOL[name][1]]

        def bcol(name):
            return bias[:, BCOL[name][0]:BCOL[name][1]]

        def ccol(name):
            return const[:, CCOL[name][0]:CCOL[name][1]]

        def hcol(name):
            return half[:, HCOL[name][0]:HCOL[name][1]]

        def block_parts(words, hidden):
            v = words.bitcast(F16)
            return v[:, 0:hidden], v[:, hidden:2 * hidden], v[:, 2 * hidden:2 * hidden + P], words[:, hidden + P // 2:]

        def block_of(layer, e):
            return block_parts(blocks[layer][:, e * layer.block:(e + 1) * layer.block], layer.H)

        first_select = block_of(L0, 0)[2]

        def tiles(ap, n=BT):
            return ap.rearrange("p (t c) -> p t c", t=n)

        def load(dst, src, name, after=()):
            return put("sync", lambda e: e.dma_start(dst, src), after, name, 16)

        def x_view(ap, s, b):
            return ap[s * SB + b].rearrange("(t p) d -> p t d", p=P)

        x_ready = [[None] * SB for _ in range(STREAMS)]
        for b in range(SB):
            x_ready[0][b] = [load(x_res[0][:, BT * b:BT * b + BT, :], x_view(x_in, 0, b), f"x_loaded0_{b}")]
        const_loaded = load(const[:, :], const_in, "const_loaded")
        weights_loaded = load(weights[:, :], w_in, "weights_loaded")
        load(half[:, :], half_in[:, 0:HALF_KEPT], "half_loaded")
        for layer in (L0, L1):
            dst = blocks[layer][:, :].bitcast(F16).rearrange("p (e c) -> p e c", e=layer.E)[:, :, 2 * layer.H:2 * layer.H + P]
            half_loaded = load(dst, half_in[:, HALF_KEPT:HALF_KEPT + layer.E * P].rearrange("p (e c) -> p e c", c=P), "half_loaded")
        for b in range(SB):
            x_ready[1][b] = [load(x_res[1][:, BT * b:BT * b + BT, :], x_view(x_in, 1, b), f"x_loaded1_{b}")]

        rows_free = [None] * STREAMS

        def zero_rows(s):
            zero = work.take()
            zeroed = put("gpsimd", lambda e: e.memset(zero.ap, 0.0), zero.ready, "zero_done")
            dst = rows_dram[s].rearrange("(n p a) c -> p n (a c)", p=P, a=BT)
            src = zero.ap.bitcast(F16).unsqueeze(1).to_broadcast([P, MAX_TILES // BT, BT * 2 * D])
            rows_free[s] = [load(dst, src, f"rows_zeroed{s}", [zeroed])]
            work.release(zero, *rows_free[s])

        def split_biases():
            raw = [work.take() for _ in range(-(-BCOLS // SEQ))]
            high = work.take()
            ready = [t for r in raw + [high] for t in r.ready]
            pieces = [(lo, min(lo + SEQ, BCOLS)) for lo in range(0, BCOLS, SEQ)]
            for r, (lo, hi) in zip(raw, pieces):
                loaded = load(r.ap[:, 0:hi - lo], bias_in[:, lo:hi], "bias_loaded", r.ready)
            clear = put("vector", lambda e: e.memset(bias[:, :], 0.0), (), "bias_step")
            scale = 1 / SEL_VALUE
            for lo, hi in pieces:
                src = raw[lo // SEQ].ap[:, lo % SEQ:lo % SEQ + hi - lo]
                top = high.ap.bitcast(F16)[:, lo:hi]
                t = put("vector", lambda e, src=src, top=top, scale=scale: e.tensor_scalar(top, src, scale, None, ALU.mult),
                        [loaded, clear] + ready, "bias_step")
                put("vector", lambda e, top=top, lo=lo, hi=hi: e.tensor_copy(bias[0:LOW_ROW, lo:hi], top[0:LOW_ROW, :]), [t], "bias_step")
                r = slice(LOW_ROW, 2 * LOW_ROW)
                t = put("vector", lambda e, src=src, top=top, lo=lo, hi=hi, scale=scale, r=r:
                        e.scalar_tensor_tensor(bias[r, lo:hi], src[r, :], scale, top[r, :], ALU.mult, ALU.subtract), [t], "bias_step")
            for r in raw + [high]:
                work.release(r, t)
            return t

        def place_hidden_biases(layer, name):
            dst = blocks[layer][:, :].rearrange("p (e c) -> p e c", e=layer.E)[:, :, layer.block - layer.chunks:layer.block]
            return put("vector", lambda e: e.tensor_copy(dst, wcol(name).rearrange("p (e c) -> p e c", e=layer.E)), [weights_loaded], "hidden_biases_placed")

        w1_ready = {}

        def split_w1(layer, source, e0, n):
            raw = work.take()
            loaded = load(raw.ap.rearrange("p (e h) -> p e h", e=n), source[e0:e0 + n].rearrange("e d h -> d e h"), raw.name, raw.ready)
            for i in range(n):
                high, low, *_ = block_of(layer, e0 + i)
                src = raw.ap[:, i * layer.H:(i + 1) * layer.H]
                t = put("scalar", lambda e: e.activation(high, src, ACT.Copy, scale=W_SCALE), [loaded], "w1_high_done")
                done = put("vector", lambda e: e.scalar_tensor_tensor(low, src, W_SCALE, high, ALU.mult, ALU.subtract), [t, loaded], "w1_low_done")
            work.release(raw, done)
            w1_ready[layer] = w1_ready[layer][:1] + [t, done]

        def layer_norm(s, b):
            sm, xn = small.take(), work.take()
            stats, mean_var, rstd = sm.ap[:, 0:24], sm.ap[:, 24:32], sm.ap[:, 32:36]
            x = x_res[s]
            for i in range(BT):
                t = put("vector", lambda e, i=i: e.bn_stats(stats[:, 6 * i:6 * i + 6], x[:, BT * b + i, :]), x_ready[s][b] + sm.ready, f"norm_stats{s}")
            for i in range(BT):
                t2 = put("vector", lambda e, i=i: e.bn_aggr(mean_var[:, 2 * i:2 * i + 2], stats[:, 6 * i:6 * i + 6]), [t], f"norm_stats{s}")
            var, sq = sm.ap[:, 36:40], sm.ap[:, 40:44]

            def step(fn):
                return put("vector", fn, [put_last[0]], f"norm_stats{s}")
            put_last = [t2]
            for fn in [lambda e: e.tensor_scalar(var, mean_var.rearrange("p (t v) -> p t v", v=2)[:, :, 1], EPS, None, ALU.add),
                       lambda e: e.tensor_scalar(rstd.bitcast(I32), var.bitcast(I32), 1, None, ALU.logical_shift_right),
                       lambda e: e.tensor_scalar(rstd.bitcast(I32), rstd.bitcast(I32), -1.0, float(RSQRT_GUESS), ALU.mult, ALU.add),
                       ] + [lambda e: e.tensor_tensor(sq, rstd, rstd, ALU.mult),
                            lambda e: e.scalar_tensor_tensor(sq, sq, -0.5, var, ALU.mult, ALU.mult),
                            lambda e: e.scalar_tensor_tensor(rstd, sq, 1.5, rstd, ALU.add, ALU.mult)] * NEWTON_STEPS:
                put_last[0] = step(fn)
            t3 = put_last[0]
            for i in range(BT):
                t4 = put("vector", lambda e, i=i: e.tensor_scalar(xn.ap[:, D * i:D * i + D], x[:, BT * b + i, :], mean_var[:, 2 * i:2 * i + 1],
                                                                 rstd[:, i:i + 1], ALU.subtract, ALU.mult), [t3] + xn.ready, f"norm_done{s}")
            small.release(sm, t4)
            return xn, t4

        def turn_batch(s, xn, xn_done):
            bk, xt = banks.take(), work.take()

            def go(e):
                for i in range(BT):
                    m = e.transpose(bk.ap[:, P * i:P * i + P], xn.ap[:, D * i:D * i + D], ccol("ident"))
                return m
            turned = put("tensor", go, [xn_done, const_loaded] + bk.ready, f"turned{s}")
            xt_done = put("scalar", lambda e: e.activation(xt.ap, bk.ap, ACT.Copy), [turned] + xt.ready, f"xt_done{s}")
            banks.release(bk, xt_done)
            return xt, xt_done, turned

        state = [dict() for _ in range(STREAMS)]

        def gate_batch(s, b, layer):
            E = layer.E
            gate_w, gate_b = (wcol("gate_w0"), wcol("gate_b0")) if layer is L0 else (wcol("gate_w1"), wcol("gate_b1"))
            st = state[s]
            scores = st["scores"]
            xn, xn_done = layer_norm(s, b)
            yield 0, 6.0
            xt, xt_done, turned = turn_batch(s, xn, xn_done)
            rows = work.take()
            parts = rows.ap.bitcast(F16).rearrange("p (t h d) -> p t h d", t=BT, h=2)
            high = put("scalar", lambda e: e.activation(parts[:, :, 0, :], tiles(xn.ap), ACT.Copy, scale=X_SCALE), [xn_done] + rows.ready, f"rows_high{s}")
            low = put("vector", lambda e: e.scalar_tensor_tensor(parts[:, :, 1, :], tiles(xn.ap), X_SCALE, parts[:, :, 0, :], ALU.mult, ALU.subtract),
                      [high], f"rows_low{s}")
            work.release(xn, turned, high, low)
            st["rows"][b] = (rows, [high, low])
            yield 0.9, 3.0
            bk = banks.take()

            def go(e):
                for i in range(BT):
                    m = e.matmul(bk.ap[:, E * i:E * i + E], xt.ap[:, P * i:P * i + P], gate_w, start=True, stop=True)
                return m
            scored = put("tensor", go, [xt_done, weights_loaded] + bk.ready, f"scored{s}")
            out = scores.ap[:, E * BT * b:E * BT * (b + 1)].rearrange("p (t e) -> p t e", t=BT)
            t = put("vector", lambda e: e.tensor_tensor(out, bk.ap[:, 0:BT * E].rearrange("p (t e) -> p t e", t=BT),
                                                        gate_b.unsqueeze(1).to_broadcast([P, BT, E]), ALU.add), [scored] + scores.ready, f"scores_done{s}")
            banks.release(bk, t)
            st["scores_done"][b] = t
            if layer is L1:
                xt_users = [scored]
                hidden = []
                for c in range(L1.chunks):
                    bk = banks.take()
                    made = put("tensor", lambda e, bk=bk, c=c: e.matmul(bk.ap, wcol("sw1")[:, P * c:P * c + P], xt.ap, start=True, stop=True),
                               [xt_done, weights_loaded] + bk.ready, f"shared_hidden{s}")
                    hs = work.take()
                    done = put("scalar", lambda e, bk=bk, c=c, hs=hs: e.activation(hs.ap, bk.ap, ACT.Gelu, bias=wcol("sb1")[:, c:c + 1]),
                               [made] + hs.ready, f"shared_gelu{s}")
                    banks.release(bk, done)
                    hidden.append((hs, done))
                    xt_users.append(made)
                work.release(xt, *xt_users)
                yield 1.8, 4.0
                bk = banks.take()

                def go(e):
                    for i in range(BT):
                        out = bk.ap[:, D * i:D * i + D]
                        e.matmul(out, first_select, bcol("sb2"), start=True, stop=False)
                        for c in range(L1.chunks):
                            m = e.matmul(out, hidden[c][0].ap[:, P * i:P * i + P], wcol("sw2")[:, D * c:D * c + D], start=False, stop=(c == L1.chunks - 1))
                    return m
                made = put("tensor", go, [h[1] for h in hidden] + [bias_ready[0], half_loaded] + bk.ready, f"shared_out{s}")
                for hs, _ in hidden:
                    work.release(hs, made)
                xb = x_res[s][:, BT * b:BT * b + BT, :]
                t = put("vector", lambda e: e.scalar_tensor_tensor(xb, tiles(bk.ap), 0.5, xb, ALU.mult, ALU.add), [made, xn_done] + x_ready[s][b], f"x_done{s}")
                banks.release(bk, t)
                x_ready[s][b] = [t]
            else:
                work.release(xt, scored)
            yield 2.5, 3.0

        def route(s, layer):
            E = layer.E
            N = E * NT
            st = state[s]
            rev = (ccol("rev0") if layer is L0 else ccol("rev1"))
            sig = f"route{s}"
            scores = st["scores"]
            sm = small.take()
            by_token = "p (t e) -> p t e"
            last = list(st["scores_done"].values()) + sm.ready + [const_loaded]

            def dve(fn, *more):
                t = put("vector", fn, last + list(more), sig)
                last[:] = [t]
                return t

            def over_t(ap):
                return ap.unsqueeze(2).to_broadcast([P, NT, E])

            def over_e(ap):
                return ap.unsqueeze(1).to_broadcast([P, NT, E])

            S = scores.ap[:, 0:N].rearrange(by_token, t=NT)
            if layer is L1:
                top, total = sm.ap[:, 0:NT], sm.ap[:, NT:2 * NT]
                dve(lambda e: e.tensor_reduce(top, S, AX.X, ALU.max))
                dve(lambda e: e.tensor_tensor(S, S, over_t(top), ALU.subtract))
                t = put("scalar", lambda e: e.activation(scores.ap[:, 0:N], scores.ap[:, 0:N], ACT.Exp), last, f"route_exp{s}")
                dve(lambda e: e.tensor_reduce(total, S, AX.X, ALU.add), t)
                dve(lambda e: e.reciprocal(total, total))
                dve(lambda e: e.tensor_tensor(S, S, over_t(total), ALU.mult))
            yield 0, (1.0 if layer is L0 else 4.0)
            one_hot, tmp = [work.take(), work.take()], work.take()
            value = [sm.ap[:, 2 * NT:3 * NT], sm.ap[:, 3 * NT:4 * NT]]
            pick = sm.ap[:, 4 * NT:5 * NT]
            T = tmp.ap[:, 0:N].rearrange(by_token, t=NT)
            for k in range(TOP_K):
                O = one_hot[k].ap[:, 0:N].rearrange(by_token, t=NT)
                dve(lambda e, k=k: e.tensor_reduce(value[k], S, AX.X, ALU.max))
                dve(lambda e, k=k: e.tensor_tensor(T, S, over_t(value[k]), ALU.is_equal), *tmp.ready)
                dve(lambda e: e.tensor_tensor(T, T, over_e(rev), ALU.mult))
                dve(lambda e: e.tensor_reduce(pick, T, AX.X, ALU.max))
                dve(lambda e, O=O: e.tensor_tensor(O, over_e(rev), over_t(pick), ALU.is_equal), *one_hot[k].ready)
                if k == 0:
                    dve(lambda e, O=O: e.scalar_tensor_tensor(S, O, -3e38, S, ALU.mult, ALU.add))
                yield 0, 3.0
            marks = work.take()
            mark = marks.ap.bitcast(F16)[:, 0:N]
            carry = marks.ap.bitcast(F16)[:, SEQ:SEQ + N]
            mark_v = mark.rearrange("p (e t) -> p t e", e=E)
            dve(lambda e: e.tensor_tensor(mark_v, one_hot[0].ap[:, 0:N].rearrange(by_token, t=NT), one_hot[1].ap[:, 0:N].rearrange(by_token, t=NT), ALU.add), *marks.ready)
            dve(lambda e: e.tensor_tensor_scan(tmp.ap[:, 0:N], ccol("carry")[:, 0:N], mark, 0.0, ALU.mult, ALU.add))
            dve(lambda e: e.tensor_tensor(carry, tmp.ap[:, 0:N], mark, ALU.subtract))
            lastc = marks.ap.bitcast(F16)[:, SEQ - 2 * L0.E:SEQ - 2 * L0.E + E]
            counted = dve(lambda e: e.tensor_copy(lastc, tmp.ap[:, 0:N].rearrange("p (e t) -> p e t", e=E)[:, :, NT - 1]))
            bk = banks.take()

            def go(e):
                e.matmul(bk.ap[:, 0:N], hcol("before"), mark, start=True, stop=False)
                e.matmul(bk.ap[:, 0:N], hcol("ones"), carry, start=False, stop=True)
                return e.matmul(bk.ap[:, N:N + E], hcol("ones"), lastc, start=True, stop=True)
            ranked = put("tensor", go, [counted, half_loaded] + bk.ready, f"ranked{s}")
            yield 0.3, 5.0
            sm2 = small.take()
            need_i = sm2.ap[:, 0:E].bitcast(I32)
            need, end, base = sm2.ap[:, E:2 * E], sm2.ap[:, 2 * E:3 * E], sm2.ap[:, 3 * E:4 * E]
            dve(lambda e: e.tensor_scalar(need_i, bk.ap[:, N:N + E], float(P - 1), None, ALU.add), ranked, *sm2.ready)
            dve(lambda e: e.tensor_scalar(need_i, need_i, P.bit_length() - 1, None, ALU.arith_shift_right))
            dve(lambda e: e.tensor_copy(need, need_i))
            dve(lambda e: e.tensor_tensor_scan(end, hcol("ones")[:, 0:E], need, 0.0, ALU.mult, ALU.add))
            dve(lambda e: e.tensor_tensor(base, end, need, ALU.subtract))
            dve(lambda e: e.tensor_scalar(base, base, float(P), None, ALU.mult))
            R = tmp.ap[:, 0:N].rearrange("p (e t) -> p e t", e=E)
            dve(lambda e: e.tensor_tensor(R, bk.ap[:, 0:N].rearrange("p (e t) -> p e t", e=E), base.unsqueeze(2).to_broadcast([P, E, NT]), ALU.add))
            banks.release(bk, last[0])
            Rt = tmp.ap[:, 0:N].rearrange("p (e t) -> p t e", e=E)
            for k in range(TOP_K):
                O = one_hot[k].ap[:, 0:N].rearrange(by_token, t=NT)
                dve(lambda e, O=O: e.tensor_tensor(O, O, Rt, ALU.mult))
                dve(lambda e, O=O: e.tensor_reduce(pick, O, AX.X, ALU.add))
                indexed = dve(lambda e, k=k: e.tensor_copy(slot_index[s][:, k, :], pick), *st.get("index_free", []))
            yield 0, 5.0
            scattered = []
            for b in range(SB):
                rows, made = st["rows"][b]
                for i in range(BT):
                    for k in range(TOP_K):
                        src = rows.ap.bitcast(F16)[:, 2 * D * i:2 * D * i + 2 * D]
                        at = slot_index[s][:, k, BT * b + i:BT * b + i + 1]
                        t = put("gpsimd", lambda e, src=src, at=at: e.indirect_dma_start(
                            rows_dram[s], bass.IndirectOffsetOnAxis(ap=at, axis=0), src, None), made + [indexed] + rows_free[s], rows.name + "_indirect", 16)
                work.release(rows, t)
                scattered.append(t)
            st["scattered"] = scattered
            ej = sm.ap[:, 0:1]
            dve(lambda e: e.tensor_scalar(need, end, ccol("iota"), None, ALU.is_le))
            dve(lambda e: e.tensor_reduce(ej, need, AX.X, ALU.add))
            named = dve(lambda e: e.tensor_scalar(ej, ej, float(E - 1), None, ALU.min))
            bk = banks.take()
            turned = put("tensor", lambda e: e.matmul(bk.ap[0:1, 0:P], ej, ccol("ident"), start=True, stop=True), [named] + bk.ready, f"ranked{s}")
            dve(lambda e: e.tensor_scalar(tile_expert[s][0:1, 0, 0:layer.tiles], bk.ap[0:1, 0:layer.tiles], float(layer.block), None, ALU.mult), turned, *st.get("expert_free", []))
            dve(lambda e: e.tensor_scalar(tile_expert[s][0:1, 1, 0:layer.tiles], bk.ap[0:1, 0:layer.tiles], 1.0, None, ALU.mult))
            banks.release(bk, last[0])
            st["experts_named"] = last[0]
            if layer is L0:
                gap = sm.ap[:, NT:2 * NT]
                t = dve(lambda e: e.tensor_tensor(gap, value[1], value[0], ALU.subtract))
                t = put("scalar", lambda e: e.activation(gap, gap, ACT.Exp), [t], f"route_exp{s}")
                dve(lambda e: e.tensor_scalar(pick, gap, 1.0, None, ALU.add), t)
                dve(lambda e: e.reciprocal(pick, pick))
                dve(lambda e: e.tensor_scalar(share[s][:, 0, :], pick, 0.5, None, ALU.mult))
                dve(lambda e: e.tensor_tensor(share[s][:, 1, :], share[s][:, 0, :], gap, ALU.mult))
            else:
                for k in range(TOP_K):
                    dve(lambda e, k=k: e.tensor_scalar(share[s][:, k, :], value[k], 0.5, None, ALU.mult))
            st["shared_out"] = last[0]
            for sl in one_hot + [tmp, marks, scores]:
                work.release(sl, last[0])
            small.release(sm, last[0])
            small.release(sm2, last[0])
            yield 0, 2.5, INDIRECT_TIME * TOP_K * NT

        def experts(s, layer):
            H, C = layer.H, layer.chunks
            st = state[s]
            groups = layer.tiles // BT
            pe_time = layer.unit * (layer.chunks * (3 + 4) + 1 + 2) * PASS_TIME
            w2_dram = (w2_0 if layer is L0 else w2_1).rearrange("e (c p) d -> p e c d", p=P)
            b2 = bcol("b2_0") if layer is L0 else bcol("b2_1")
            turned_rows = {}
            rows_read = []
            block_at, w2_at = {}, {}

            def read_tile_experts(g):
                if g % LOAD_GROUPS:
                    return
                n = min(LOAD_GROUPS, groups - g) * BT
                for row, engine, values, top in ((0, VECTOR, block_at, (layer.E - 1) * layer.block), (1, SYNC, w2_at, layer.E - 1)):
                    put(engine, lambda e: None, [st["experts_named"]])
                    _, regs = nc.values_load_multi_w_load_instructions(
                        tile_expert[s][0:1, row, BT * g:BT * g + n], engines=[ENGINE_TYPE[engine]], min_val=0, max_val=top, skip_runtime_bounds_check_because="the counts keep them in range")
                    for i, r in enumerate(regs):
                        values[BT * g + i] = r

            def bring_weights(unit):
                blk, second = block_slots.take(), work.take()
                for j in range(layer.unit):
                    tile = unit * layer.unit + j
                    dst = blk.ap[:, j * layer.block:(j + 1) * layer.block]
                    copied = put("vector", lambda e: e.tensor_copy(dst, blocks[layer][:, bass.ds(block_at[tile], layer.block)]),
                                 w1_ready[layer] + [half_loaded] + blk.ready, f"block_copied{s}")
                    dst2 = second.ap[:, j * H:(j + 1) * H].rearrange("p (o c d) -> p o c d", o=1, c=C)
                    landed = load(dst2, w2_dram[:, bass.ds(w2_at[tile], 1)], second.name, second.ready)
                return blk, copied, second, landed

            def fetch(g):
                rows = work.take()
                src = rows_dram[s][g * BT * P:(g + 1) * BT * P].rearrange("(t p) c -> p t c", p=P)
                t = load(rows.ap.bitcast(F16).rearrange("p (t c) -> p t c", t=BT), src, rows.name, st["scattered"] + rows.ready)
                rows_read.append(t)
                return rows, t

            def turn(g, rows, loaded):
                bk, xt = turn_banks.take(), work.take()
                R = rows.ap.bitcast(F16).rearrange("p (n d) -> p n d", d=D)

                def go(e):
                    for n in range(2 * BT):
                        m = e.transpose(bk.ap[:, P * n:P * n + P], R[:, n, :], hcol("ident"))
                    return m
                turned = put("tensor", go, [loaded, half_loaded] + bk.ready, f"rows_turned{s}")
                work.release(rows, turned)
                done = put("scalar", lambda e: e.activation(xt.ap.bitcast(F16), bk.ap, ACT.Copy), [turned] + xt.ready, f"rows_xt{s}")
                turn_banks.release(bk, done)
                turned_rows[g] = (xt, done)

            yield FILLER
            def store_group(g, out_bank, done):
                y = work.take()
                copied = put("scalar", lambda e: e.activation(y.ap, out_bank.ap, ACT.Copy), [done] + y.ready, f"y_copied{s}")
                out_banks.release(out_bank, copied)
                dst = y_dram[s][g * BT * P:(g + 1) * BT * P].rearrange("(t p) d -> p t d", p=P)
                y_stored = put("sync", lambda e: e.dma_start(dst, tiles(y.ap)), [copied] + st.get("y_free", []), y.name, 16)
                work.release(y, y_stored)
                users.append(y_stored)

            full = []
            fetched = [fetch(0), fetch(1)]
            read_tile_experts(0)
            brought = [bring_weights(unit) for unit in range(WEIGHTS_AHEAD)]
            units = layer.tiles // layer.unit
            turn(0, *fetched[0])
            pending = []
            out_bank = None
            users = []
            for unit in range(units):
                first = unit * layer.unit
                g = first // BT
                if first % BT == 0:
                    if g + 2 < groups:
                        fetched.append(fetch(g + 2))
                xt, xt_done = turned_rows[g]
                hb, hid = hidden_banks.take(), work.take()

                blk, copied, second, landed = brought[unit]

                def layer1(e):
                    X = xt.ap.bitcast(F16).rearrange("p (t h n) -> p t h n", t=BT, h=2)
                    for j in range(layer.unit):
                        xh, xl = X[:, (first + j) % BT, 0, :], X[:, (first + j) % BT, 1, :]
                        high, low, *_ = block_parts(blk.ap[:, j * layer.block:(j + 1) * layer.block], H)
                        for c in range(C):
                            out = hb.ap[:, j * H + c * P:j * H + c * P + P]
                            e.matmul(out, high[:, c * P:c * P + P], xh, start=True, stop=False)
                            e.matmul(out, high[:, c * P:c * P + P], xl, start=False, stop=False)
                            m = e.matmul(out, low[:, c * P:c * P + P], xh, start=False, stop=True)
                    return m
                made = put("tensor", layer1, [xt_done, copied] + hb.ready, f"hidden_made{s}")
                if (first + layer.unit) % BT == 0:
                    work.release(xt, made)

                def activate(e):
                    for j in range(layer.unit):
                        b1 = block_parts(blk.ap[:, j * layer.block:(j + 1) * layer.block], H)[3]
                        for c in range(C):
                            at = slice(j * H + c * P, j * H + c * P + P)
                            m = e.activation(hid.ap[:, at], hb.ap[:, at], ACT.Gelu, bias=b1[:, c:c + 1], scale=1 / (X_SCALE * W_SCALE))
                    return m
                gelu = put("scalar", activate, [made, copied] + hid.ready, f"hidden_gelu{s}")
                hidden_banks.release(hb, gelu)
                if first % BT == 0 and g + 1 < groups:
                    turn(g + 1, *fetched[g + 1])
                pending.append((first, hid, gelu, brought[unit]))
                ripe, pending = (pending[:-HIDDEN_AHEAD], pending[-HIDDEN_AHEAD:]) if unit < units - 1 else (pending, [])
                for first2, hid2, gelu2, (blk2, copied2, second2, landed2) in ripe:
                    if first2 % BT == 0:
                        out_bank = out_banks.take()

                    def layer2(e):
                        for j in range(layer.unit):
                            out = out_bank.ap[:, D * ((first2 + j) % BT):D * ((first2 + j) % BT) + D]
                            select = block_parts(blk2.ap[:, j * layer.block:(j + 1) * layer.block], H)[2]
                            e.matmul(out, select, b2, start=True, stop=False)
                            for c in range(C):
                                at = slice(j * H + c * P, j * H + c * P + P)
                                m = e.matmul(out, hid2.ap[:, at], second2.ap[:, at], start=False, stop=(c == C - 1))
                        return m
                    done = put("tensor", layer2, [gelu2, landed2, copied2, bias_ready[0]] + out_bank.ready, f"expert_out{s}")
                    block_slots.release(blk2, done)
                    work.release(second2, done)
                    work.release(hid2, done)
                    if (first2 + layer.unit) % BT == 0:
                        full.append((first2 // BT, out_bank, done, unit))
                while full and (full[0][3] < unit or unit == units - 1):
                    store_group(*full.pop(0)[:3])
                if unit + WEIGHTS_AHEAD < units:
                    if (unit + WEIGHTS_AHEAD) * layer.unit % BT == 0:
                        read_tile_experts((unit + WEIGHTS_AHEAD) * layer.unit // BT)
                    brought.append(bring_weights(unit + WEIGHTS_AHEAD))
                yield pe_time, pe_time
            rows_free[s] = rows_read
            st["expert_free"] = [brought[-1][1], brought[-1][3]]
            st["y_stored"] = users
            st["y_free"], st["index_free"] = [], []

        def combine_batch(s, b):
            st = state[s]
            x = x_res[s]
            yield GPSIMD_IDLE
            gathered = []
            for pair in range(BT // 2):
                got = work.take()
                for i in range(2):
                    for k in range(TOP_K):
                        t, col = BT * b + 2 * pair + i, D * (2 * i + k)
                        at = slot_index[s][:, k, t:t + 1]
                        landed = put("gpsimd", lambda e, got=got, col=col, at=at: e.indirect_dma_start(
                            got.ap[:, col:col + D], None, y_dram[s], bass.IndirectOffsetOnAxis(ap=at, axis=0)),
                            st["y_stored"] + got.ready, got.name + "_indirect", 16)
                        gathered.append((t, k, got, col))
                got.landed = landed
                st["y_free"].append(landed)
                st["index_free"].append(landed)
            yield 0, 2.5, INDIRECT_TIME * TOP_K * BT
            for t, k, got, col in gathered:
                done = put("vector", lambda e, t=t, k=k, col=col, got=got: e.scalar_tensor_tensor(
                    x[:, t, :], got.ap[:, col:col + D], share[s][:, k, t:t + 1], x[:, t, :], ALU.mult, ALU.add),
                    [got.landed, st["shared_out"]] + x_ready[s][b], f"x_done{s}")
                x_ready[s][b] = [done]
                if col == SEQ - D:
                    work.release(got, done)
            yield 0, 2.0

        def linear_attention(s, b):
            xn, xn_done = layer_norm(s, b)
            yield 0, 6.0
            xt, xt_done, turned = turn_batch(s, xn, xn_done)
            work.release(xn, turned)
            yield 0.9, 3.0
            first = {}
            for name, mat, bi in (("q", "q1", "q_b1"), ("k", "k1", "k_b1"), ("v", "v", "v_b"), ("g", "g", "g_b")):
                bk, out = banks.take(), work.take()
                made = put("tensor", lambda e, bk=bk, mat=mat: e.matmul(bk.ap, wcol(mat), xt.ap, start=True, stop=True),
                           [xt_done, weights_loaded] + bk.ready, f"attn_made{s}")
                done = put("scalar", lambda e, bk=bk, out=out, bi=bi: e.activation(out.ap, bk.ap, ACT.Gelu, bias=wcol(bi)), [made] + out.ready, f"attn_gelu{s}")
                banks.release(bk, done)
                first[name] = (out, done)
                if name == "k":
                    yield 1.7, 2.0
            work.release(xt, made)
            yield 1.7, 3.0
            second = {}
            zs = []
            for name, mat, bi in (("q", "q2", "q_b2"), ("k", "k2", "k_b2")):
                hid, hid_done = first[name]
                bk, z, mag = banks.take(), work.take(), work.take()

                def go(e, bk=bk, hid=hid, mat=mat, bi=bi):
                    for i in range(BT):
                        out = bk.ap[:, D * i:D * i + D]
                        e.matmul(out, first_select, bcol(bi), start=True, stop=False)
                        m = e.matmul(out, hid.ap[:, P * i:P * i + P], wcol(mat), start=False, stop=True)
                    return m
                made = put("tensor", go, [hid_done, bias_ready[0], half_loaded] + bk.ready, f"attn_made{s}")
                work.release(hid, made)
                pos = put("vector", lambda e, bk=bk, z=z: e.tensor_scalar(z.ap, bk.ap, 0.0, None, ALU.max), [made] + z.ready, f"attn_dve{s}")
                size = put("vector", lambda e, bk=bk, z=z, mag=mag: e.scalar_tensor_tensor(mag.ap, z.ap, -2.0, bk.ap, ALU.mult, ALU.add),
                           [pos] + mag.ready, f"attn_dve{s}")
                banks.release(bk, size)
                zs.append((name, z, mag, size))
            yield 1.0, 3.0
            exps = []
            for name, z, mag, size in zs:
                exps.append(put("scalar", lambda e, mag=mag: e.activation(mag.ap, mag.ap, ACT.Exp), [size], f"attn_exp{s}"))
            for (name, z, mag, size), ex in zip(zs, exps):
                ln = put("scalar", lambda e, mag=mag: e.activation(mag.ap, mag.ap, ACT.Ln, bias=ccol("one")), [ex, const_loaded], f"attn_exp{s}")
                done = put("vector", lambda e, z=z, mag=mag: e.tensor_tensor(z.ap, z.ap, mag.ap, ALU.add), [ln], f"attn_dve{s}")
                work.release(mag, done)
                second[name] = (z, done)
            yield 1.0, 4.0
            (qs, q_done), (ks, k_done) = second["q"], second["k"]
            bk, sm, at_ = banks.take(), small.take(), work.take()

            def go(e):
                for i in range(BT):
                    m = e.matmul(bk.ap[:, 0:D], ks.ap[:, D * i:D * i + D], qs.ap[:, D * i:D * i + D], start=(i == 0), stop=(i == BT - 1))
                return m
            made = put("tensor", go, [q_done, k_done] + bk.ready, f"attn_made{s}")
            work.release(qs, made)
            work.release(ks, made)
            heads = at_.ap[:, 0:D]
            masked = put("vector", lambda e: e.tensor_tensor(heads, bk.ap[:, 0:D], ccol("heads"), ALU.mult), [made, const_loaded] + at_.ready, f"attn_dve{s}")
            banks.release(bk, masked)
            yield 0.9, 2.0
            (vt, v_done), (gt, g_done) = first["v"], first["g"]
            bk, bk2 = banks.take(), banks.take()
            summed = put("tensor", lambda e: e.matmul(bk2.ap[:, 0:1], heads, ccol("one"), start=True, stop=True), [masked] + bk2.ready, f"attn_made{s}")
            made = put("tensor", lambda e: e.matmul(bk.ap, heads, vt.ap, start=True, stop=True), [v_done] + bk.ready, f"attn_made{s}")
            z1, z2 = sm.ap[:, 0:1], sm.ap[:, 1:2]
            t = put("vector", lambda e: e.tensor_scalar(z1, bk2.ap[:, 0:1], float(D), None, ALU.add), [summed] + sm.ready, f"attn_dve{s}")
            banks.release(bk2, t)
            zinv = put("vector", lambda e: e.reciprocal(z2, z1), [t], f"attn_dve{s}")
            t = put("vector", lambda e: e.tensor_tensor(vt.ap, bk.ap, vt.ap, ALU.add), [made], f"attn_dve{s}")
            banks.release(bk, t)
            work.release(at_, made)
            o = work.take()
            o_view = o.ap.rearrange("p (c a) -> p a c", a=SEQ // HEADS)
            gated = put("vector", lambda e: e.scalar_tensor_tensor(o_view, vt.ap.rearrange("p (a c) -> p a c", c=HEADS), z2,
                                                                   gt.ap.rearrange("p (a c) -> p a c", c=HEADS), ALU.mult, ALU.mult),
                        [t, zinv, g_done] + o.ready, f"attn_dve{s}")
            small.release(sm, gated)
            work.release(vt, gated)
            work.release(gt, gated)
            hd = heads_dram[s * SB + b]
            stored = put("sync", lambda e: e.dma_start(hd.rearrange("c p a -> p c a"), o.ap.rearrange("p (c a) -> p c a", c=HEADS)), [gated], o.name, 16)
            work.release(o, stored)
            m = work.take()
            landed = load(m.ap, hd.rearrange("c (n h) a -> (c n) (h a)", h=HEADS), m.name, [stored] + m.ready)
            yield 1.1, 12.0
            bk = banks.take()

            def go2(e):
                for i in range(BT):
                    out = bk.ap[:, D * i:D * i + D]
                    e.matmul(out, first_select, bcol("p_b"), start=True, stop=False)
                    mm = e.matmul(out, m.ap[:, P * i:P * i + P], wcol("p"), start=False, stop=True)
                return mm
            made = put("tensor", go2, [landed] + bk.ready, f"attn_made{s}")
            work.release(m, made)
            xb = x_res[s][:, BT * b:BT * b + BT, :]
            t = put("vector", lambda e: e.tensor_tensor(xb, tiles(bk.ap), xb, ALU.add), [made, xn_done] + x_ready[s][b], f"x_done{s}")
            banks.release(bk, t)
            x_ready[s][b] = [t]
            yield 1.0, 2.0

        def causal_attention(s, b):
            xn, xn_done = layer_norm(s, b)
            yield 0, 6.0
            xt, xt_done, turned = turn_batch(s, xn, xn_done)
            work.release(xn, turned)
            yield 0.9, 3.0
            roped = []
            for mat in ("wq", "wk"):
                parts = []
                for m_name, table in ((mat, "cos"), (mat + "_swap", "sin")):
                    bk, out = banks.take(), work.take()
                    made = put("tensor", lambda e, bk=bk, m_name=m_name: e.matmul(bk.ap, wcol(m_name), xt.ap, start=True, stop=True),
                               [xt_done, weights_loaded] + bk.ready, f"attn_made{s}")
                    done = put("vector", lambda e, bk=bk, out=out, table=table: e.tensor_tensor(out.ap, bk.ap, ccol(table), ALU.mult),
                               [made, const_loaded] + out.ready, f"attn_dve{s}")
                    banks.release(bk, done)
                    parts.append((out, done))
                (a, a_done), (c, c_done) = parts
                done = put("vector", lambda e, a=a, c=c: e.tensor_tensor(a.ap, a.ap, c.ap, ALU.add), [a_done, c_done], f"roped{s}")
                work.release(c, done)
                roped.append((a, done))
                yield 1.7, 2.5
            bk, v = banks.take(), work.take()

            def go(e):
                for i in range(BT):
                    m = e.matmul(bk.ap[:, D * i:D * i + D], xt.ap[:, P * i:P * i + P], wcol("wv"), start=True, stop=True)
                return m
            made = put("tensor", go, [xt_done] + bk.ready, f"attn_made{s}")
            work.release(xt, made)
            v_done = put("scalar", lambda e: e.activation(v.ap, bk.ap, ACT.Copy), [made] + v.ready, f"attn_copy{s}")
            banks.release(bk, v_done)
            yield 0.9, 1.5
            (qt, q_done), (kt, k_done) = roped
            sm = small.take()
            for i in range(BT):
                n = P * (i + 1)
                top, neg, total, inv = (sm.ap[:, 4 * i + j:4 * i + j + 1] for j in range(4))
                bk, pr = banks.take(), work.take()
                made = put("tensor", lambda e, bk=bk, i=i, n=n: e.matmul(bk.ap[:, 0:n], qt.ap[:, P * i:P * i + P], kt.ap[:, 0:n], start=True, stop=True),
                           [q_done, k_done] + bk.ready, f"attn_made{s}")
                diag = bk.ap[:, P * i:n]
                t = put("vector", lambda e, diag=diag: e.tensor_tensor(diag, diag, ccol("causal"), ALU.add), [made], f"attn_dve{s}")
                t = put("vector", lambda e, bk=bk, n=n, top=top: e.tensor_reduce(top, bk.ap[:, 0:n], AX.X, ALU.max), [t] + sm.ready, f"attn_dve{s}")
                t = put("vector", lambda e, top=top, neg=neg: e.tensor_scalar(neg, top, -ATTN_SCALE, None, ALU.mult), [t], f"attn_dve{s}")
                ex = put("scalar", lambda e, bk=bk, pr=pr, n=n, neg=neg, total=total: e.activation(
                    pr.ap[:, 0:n], bk.ap[:, 0:n], ACT.Exp, bias=neg, scale=ATTN_SCALE, accum_out=total), [t] + pr.ready, f"attn_exp{s}")
                banks.release(bk, ex)
                yield 0.6, 4.0
                bk, prt = banks.take(), work.take()

                def go(e, bk=bk, pr=pr, i=i):
                    for j in range(i + 1):
                        m = e.transpose(bk.ap[:, P * j:P * j + P], pr.ap[:, P * j:P * j + P], ccol("ident"))
                    return m
                turned = put("tensor", go, [ex] + bk.ready, f"attn_made{s}")
                work.release(pr, turned)
                copied = put("scalar", lambda e, bk=bk, prt=prt, n=n: e.activation(prt.ap[:, 0:n], bk.ap[:, 0:n], ACT.Copy), [turned] + prt.ready, f"attn_copy{s}")
                banks.release(bk, copied)
                r = put("vector", lambda e, total=total, inv=inv: e.reciprocal(inv, total), [ex], f"attn_dve{s}")
                yield 0.5, 3.0
                bk = banks.take()

                def go(e, bk=bk, prt=prt, i=i):
                    for j in range(i + 1):
                        m = e.matmul(bk.ap[:, 0:D], prt.ap[:, P * j:P * j + P], v.ap[:, D * j:D * j + D], start=(j == 0), stop=(j == i))
                    return m
                made = put("tensor", go, [copied, v_done] + bk.ready, f"attn_made{s}")
                work.release(prt, made)
                xi = x_res[s][:, BT * b + i, :]
                t = put("vector", lambda e, bk=bk, xi=xi, inv=inv: e.scalar_tensor_tensor(xi, bk.ap[:, 0:D], inv, xi, ALU.mult, ALU.add),
                        [made, r, xn_done] + x_ready[s][b], f"x_done{s}")
                banks.release(bk, t)
                yield 0.5, 0.5
            x_ready[s][b] = [t]
            small.release(sm, t)
            for sl in (qt, kt, v):
                work.release(sl, made)

        bias_ready = [None]

        def prepare_weights():
            yield 0, 20.0
            bias_ready[0] = split_biases()
            for layer, name in ((L0, "b1_0"), (L1, "b1_1")):
                w1_ready[layer] = [place_hidden_biases(layer, name)]
            yield 0, 5.0
            for e in range(L0.E):
                split_w1(L0, w1_0, e, 1)
                yield 0, 1.6
                if e in (5, 12):
                    zero_rows((5, 12).index(e))
            yield 0, 200.0
            for e in range(0, L1.E, L1.unit):
                split_w1(L1, w1_1, e, L1.unit)
                yield 0, 4.0

        def batch(s, b, *parts):
            for part, *args in parts:
                yield from part(s, b, *args)

        def new_scores(s):
            state[s]["scores"], state[s]["rows"], state[s]["scores_done"] = work.take(), {}, {}

        def store_batch(s, b):
            put("sync", lambda e: e.dma_start(x_view(x_out, s, b), x_res[s][:, BT * b:BT * b + BT, :]), x_ready[s][b], "x_stored", 16)
            yield 0, 0

        def stream(s):
            yield 0, STREAM_DELAY * s
            for layer, *before in ((L0,), (L0, (combine_batch,), (linear_attention,)), (L1, (combine_batch,)),
                                   (L1, (combine_batch,), (causal_attention,))):
                new_scores(s)
                yield [batch(s, b, *before, (gate_batch, layer)) for b in range(SB)]
                yield from route(s, layer)
                yield from experts(s, layer)
                yield URGENT
                yield 0, 3.0
            yield 0, (1 - s) * LAST_COMBINE_DELAY
            yield [batch(s, b, (combine_batch,), (store_batch,)) for b in range(SB)]

        interleave([stream(0), stream(1), prepare_weights()], work)

        written = [Token(name, q.count[name]) for name in q.sems if name.startswith("work") or name in ("x_stored", "rows_zeroed0", "rows_zeroed1")]
        put("sync", lambda e: None, written)


def constants():
    f = np.float32
    c = np.zeros((P, CCOLS), f)

    def put(name, value):
        c[:, CCOL[name][0]:CCOL[name][1]] = value
    r = np.arange(P)
    put("ident", np.eye(P, dtype=f))
    put("heads", (r[:, None] % HEADS == r[None, :] % HEADS) * f(HEAD_SCALE))
    put("causal", np.where(r[None, :] > r[:, None], f(-1e30), f(0)))
    inv_freq = f(1) / f(10000.0) ** (np.arange(0, D, 2, dtype=f) / f(D))
    freqs = np.arange(SEQ, dtype=f)[:, None] * inv_freq
    put("cos", np.repeat(np.cos(freqs), 2, axis=-1).T)
    put("sin", np.repeat(np.sin(freqs), 2, axis=-1).T * np.where(r % 2 == 0, f(-1), f(1))[:, None])
    put("carry", np.tile((np.arange(NT) > 0).astype(f), L0.E)[None, :])
    put("rev0", (L0.E - np.arange(L0.E)).astype(f)[None, :])
    put("rev1", (L1.E - np.arange(L1.E)).astype(f)[None, :])
    put("iota", r[:, None])
    put("one", 1)
    h = np.zeros((P, HCOLS), np.float16)
    h[:, HCOL["ident"][0]:HCOL["ident"][1]] = np.eye(P)
    h[:, HCOL["before"][0]:HCOL["before"][1]] = r[:, None] < r[None, :]
    h[:, HCOL["ones"][0]:HCOL["ones"][1]] = 1
    sel = np.zeros((P, L0.E, P), np.float16)
    for e in range(L0.E):
        sel[e, e, :] = sel[LOW_ROW + e, e, :] = SEL_VALUE
    h[:, HCOL["select"][0]:HCOL["select"][1]] = sel.reshape(P, -1)
    return c, h


def kernel(**inputs):
    import concourse.bacc as bacc
    from concourse.bass_utils import run_bass_kernel_spmd

    a = {k: np.asarray(v) for k, v in inputs.items()}
    swap = np.arange(D) ^ 1
    turn = np.arange(D).reshape(HEADS, HEAD_DIM).T.ravel()
    mats = {"q1": a["L0_attn_q_w1"], "k1": a["L0_attn_k_w1"], "v": a["L0_attn_v_w"][turn], "g": a["L0_attn_g_w"][turn],
            "q2": a["L0_attn_q_w2"][turn], "k2": a["L0_attn_k_w2"][turn], "p": a["L0_attn_p_w"],
            "wq": a["L1_attn_wq"], "wq_swap": a["L1_attn_wq"][swap], "wk": a["L1_attn_wk"], "wk_swap": a["L1_attn_wk"][swap],
            "wv": a["L1_attn_wv"]}
    w = np.zeros((P, WCOLS), np.float32)
    for name, m in mats.items():
        w[:, WCOL[name][0]:WCOL[name][1]] = m.T
    for name, m in (("gate_w0", a["L0_ffn_gate_w"]), ("gate_w1", a["L1_ffn_router_w"]),
                    ("gate_b0", a["L0_ffn_gate_b"][None, :]), ("gate_b1", a["L1_ffn_router_b"][None, :]), ("sw1", a["L1_ffn_sw1"]),
                    ("sw2", a["L1_ffn_sw2"].reshape(L1.chunks, P, D).transpose(1, 0, 2).reshape(P, -1)),
                    ("q_b1", a["L0_attn_q_b1"][:, None]), ("k_b1", a["L0_attn_k_b1"][:, None]), ("v_b", a["L0_attn_v_b"][turn][:, None]),
                    ("g_b", a["L0_attn_g_b"][turn][:, None]), ("sb1", a["L1_ffn_sb1"].reshape(L1.chunks, P).T),
                    ("b1_0", a["L0_ffn_b1"].reshape(-1, P).T), ("b1_1", a["L1_ffn_rb1"].reshape(-1, P).T)):
        w[:, WCOL[name][0]:WCOL[name][1]] = m
    rows = np.zeros((P, BCOLS), np.float32)
    for name, m in (("b2_0", a["L0_ffn_b2"]), ("b2_1", a["L1_ffn_rb2"]),
                    ("q_b2", a["L0_attn_q_b2"][turn][None, :]), ("k_b2", a["L0_attn_k_b2"][turn][None, :]), ("p_b", a["L0_attn_p_b"][None, :]),
                    ("sb2", a["L1_ffn_sb2"][None, :])):
        for at in (0, LOW_ROW):
            rows[at:at + m.shape[0], BCOL[name][0]:BCOL[name][1]] = m
    c, h = constants()
    arrays = {"x": a["L0_attn_x"], "w": w, "bias_rows": rows, "const": c, "half": h, "w1_0": a["L0_ffn_w1"], "w2_0": a["L0_ffn_w2"],
              "w1_1": a["L1_ffn_rw1"], "w2_1": a["L1_ffn_rw2"]}
    arrays = {f"in_{k}_dram": np.ascontiguousarray(v) for k, v in arrays.items()}
    nc = bacc.Bacc("TRN2", target_bir_lowering=False, num_devices=1)
    args = [nc.dram_tensor(k, v.shape, mybir.dt.from_np(v.dtype), kind="ExternalInput").ap() for k, v in arrays.items()]
    args.append(nc.dram_tensor("out_0_dram", (BATCHES, SEQ, D), F32, kind="ExternalOutput").ap())
    macaron_program(nc, *args)
    r = run_bass_kernel_spmd(nc, [arrays], core_ids=[0])
    return r.results[0]["out_0_dram"]
```
